# Optimizing a Trainium2 kernel written in Bass

```python
import numpy as np
import jax
import jax.numpy as jnp

def _softmax(x, axis=-1):
    return jax.nn.softmax(x, axis=axis)

def _gelu(x):
    return jax.nn.gelu(x, approximate=True)

def _silu(x):
    return jax.nn.silu(x)

def _sigmoid(x):
    return jax.nn.sigmoid(x)

def _layernorm(x, axis=-1, eps=1e-05):
    m = jnp.mean(x, axis=axis, keepdims=True)
    v = jnp.var(x, axis=axis, keepdims=True)
    return (x - m) / jnp.sqrt(v + eps)

def _scatter_add(tgt, idx, src, axis=0):
    return tgt.at[idx].add(src)

def _segment_sum(src, seg, n):
    return jax.ops.segment_sum(src, seg, n)
kernel_name = 'mk_sandwich_d1_jaxref_r4_185ccd'

def setup_inputs(seed: int=0):
    np.random.seed(seed)
    _w = jnp.asarray

    def _L0_attn_setup():
        import jax, jax.numpy as jnp
        import numpy as np
        EMBED = 1024
        HEADS = 16
        HEAD_DIM = EMBED // HEADS
        ROT = 64
        B, S = (1, 512)
        MASK_VAL = -1000000000.0

        def _rotate_every_two(x):
            r = jnp.stack((x[..., 1::2], x[..., ::2]), axis=-1)
            return r.reshape(x.shape)

        def _fixed_pos_embedding(seq_len, rot_dim):
            inv_freq = 1.0 / 10000.0 ** (jnp.arange(0, rot_dim, 2, dtype=jnp.float32) / rot_dim)
            t = jnp.arange(seq_len, dtype=jnp.float32)
            sinusoid = jnp.einsum('i,j->ij', t, inv_freq)
            return (jnp.sin(sinusoid), jnp.cos(sinusoid))

        def _apply_rotary(x, sin, cos):
            sin = jnp.repeat(sin[None, :, None, :], 2, axis=3)
            cos = jnp.repeat(cos[None, :, None, :], 2, axis=3)
            return x * cos + _rotate_every_two(x) * sin
        key = jax.random.key(seed)
        ks = jax.random.split(key, 5)
        sc = 0.02
        return {'hidden_states': jax.random.normal(ks[0], (B, S, EMBED), jnp.float32), 'Wq': jax.random.normal(ks[1], (EMBED, EMBED), jnp.float32) * sc, 'Wk': jax.random.normal(ks[2], (EMBED, EMBED), jnp.float32) * sc, 'Wv': jax.random.normal(ks[3], (EMBED, EMBED), jnp.float32) * sc, 'Wo': jax.random.normal(ks[4], (EMBED, EMBED), jnp.float32) * sc}
    _L0_attn_in = _L0_attn_setup()

    def _L0_ffn_setup():
        import jax, jax.numpy as jnp
        import numpy as np
        ALPHA = 32
        R = 16
        SCALING = ALPHA / R
        key = jax.random.key(seed)
        k1, k2, k3, k4 = jax.random.split(key, 4)
        B_, S, D = (4, 512, 1024)
        H, r, O = (8, R, 1024)
        x = jax.random.normal(k1, (B_, S, D), dtype=jnp.float32)
        A = jax.random.normal(k2, (H, r, D), dtype=jnp.float32) * 0.02
        Bm = jax.random.normal(k3, (H, O, r), dtype=jnp.float32) * 0.02
        Wr = jax.random.normal(k4, (H, D), dtype=jnp.float32) * 0.02
        br = jnp.zeros((H,), dtype=jnp.float32)
        return {'x': x, 'A': A, 'B': Bm, 'Wr': Wr, 'br': br}
    _L0_ffn_in = _L0_ffn_setup()
    _d = {'L0_attn_hidden_states': _L0_attn_in['hidden_states'], 'L0_attn_Wq': _L0_attn_in['Wq'], 'L0_attn_Wk': _L0_attn_in['Wk'], 'L0_attn_Wv': _L0_attn_in['Wv'], 'L0_attn_Wo': _L0_attn_in['Wo'], 'L0_ffn_A': _L0_ffn_in['A'], 'L0_ffn_B': _L0_ffn_in['B'], 'L0_ffn_Wr': _L0_ffn_in['Wr'], 'L0_ffn_br': _L0_ffn_in['br']}
    _x0 = _d['L0_attn_hidden_states']
    _d['L0_attn_hidden_states'] = jax.random.normal(jax.random.fold_in(jax.random.key(seed), 1), (4, 512, 1024), dtype=_x0.dtype)
    del _x0
    return _d

def reference(L0_attn_hidden_states, L0_attn_Wq, L0_attn_Wk, L0_attn_Wv, L0_attn_Wo, L0_ffn_A, L0_ffn_B, L0_ffn_Wr, L0_ffn_br):

    def _L0_attn_ref(hidden_states, Wq, Wk, Wv, Wo):
        import jax, jax.numpy as jnp
        import numpy as np
        EMBED = 1024
        HEADS = 16
        HEAD_DIM = EMBED // HEADS
        ROT = 64
        B, S = (1, 512)
        MASK_VAL = -1000000000.0

        def _rotate_every_two(x):
            r = jnp.stack((x[..., 1::2], x[..., ::2]), axis=-1)
            return r.reshape(x.shape)

        def _fixed_pos_embedding(seq_len, rot_dim):
            inv_freq = 1.0 / 10000.0 ** (jnp.arange(0, rot_dim, 2, dtype=jnp.float32) / rot_dim)
            t = jnp.arange(seq_len, dtype=jnp.float32)
            sinusoid = jnp.einsum('i,j->ij', t, inv_freq)
            return (jnp.sin(sinusoid), jnp.cos(sinusoid))

        def _apply_rotary(x, sin, cos):
            sin = jnp.repeat(sin[None, :, None, :], 2, axis=3)
            cos = jnp.repeat(cos[None, :, None, :], 2, axis=3)
            return x * cos + _rotate_every_two(x) * sin
        b, s, e = hidden_states.shape
        q = (hidden_states @ Wq).reshape(b, s, HEADS, HEAD_DIM)
        k = (hidden_states @ Wk).reshape(b, s, HEADS, HEAD_DIM)
        v = (hidden_states @ Wv).reshape(b, s, HEADS, HEAD_DIM)
        sin, cos = _fixed_pos_embedding(s, ROT)
        q = jnp.concatenate([_apply_rotary(q[..., :ROT], sin, cos), q[..., ROT:]], axis=-1)
        k = jnp.concatenate([_apply_rotary(k[..., :ROT], sin, cos), k[..., ROT:]], axis=-1)
        q = q.transpose(0, 2, 1, 3)
        k = k.transpose(0, 2, 1, 3)
        v = v.transpose(0, 2, 1, 3)
        logits = jnp.einsum('bhqd,bhkd->bhqk', q, k)
        causal = jnp.tril(jnp.ones((s, s), dtype=bool))[None, None]
        logits = jnp.where(causal, logits, MASK_VAL)
        logits = logits / jnp.sqrt(jnp.float32(HEAD_DIM))
        attn = jax.nn.softmax(logits, axis=-1)
        out = jnp.einsum('bhqk,bhkd->bhqd', attn, v)
        out = out.transpose(0, 2, 1, 3).reshape(b, s, e)
        return out @ Wo

    def _L0_ffn_ref(x, A, B, Wr, br):
        import jax, jax.numpy as jnp
        import numpy as np
        ALPHA = 32
        R = 16
        SCALING = ALPHA / R
        H = A.shape[0]
        router_logits = jnp.einsum('bsd,hd->bsh', x, Wr) + br
        scores = H * jax.nn.softmax(router_logits, axis=-1)
        low = jnp.einsum('bsd,hrd->bshr', x, A)
        out = jnp.einsum('bshr,hor,bsh->bso', low, B, scores)
        return SCALING * out
    x = L0_attn_hidden_states
    x = x + _layernorm(_L0_attn_ref(_layernorm(x, axis=-1), L0_attn_Wq, L0_attn_Wk, L0_attn_Wv, L0_attn_Wo), axis=-1)
    x = x + _layernorm(_L0_ffn_ref(_layernorm(x, axis=-1), L0_ffn_A, L0_ffn_B, L0_ffn_Wr, L0_ffn_br), axis=-1)
    return x

_drawn_inputs = setup_inputs


def setup_inputs(seed=0):
    import zlib

    import numpy as np

    out = dict(_drawn_inputs(seed))
    spreads = {'L0_ffn_br': (0.0, 0.1)}
    factors = {}
    for name, (base, spread) in spreads.items():
        noise = np.random.default_rng([zlib.crc32(name.encode()), seed]).standard_normal(out[name].shape)
        drawn = base * np.exp(spread * noise) if base else spread * noise
        out[name] = jnp.asarray(drawn.astype(out[name].dtype))
    for name, factor in factors.items():
        out[name] = (out[name] * factor).astype(out[name].dtype)
    return out
```

```python
from contextlib import ExitStack

import concourse.bass as bass
from concourse import mybir

F32 = mybir.dt.float32
F32R = mybir.dt.float32r
ALU = mybir.AluOpType
ACT = mybir.ActivationFunctionType
AX = mybir.AxisListType

P = 128
EMBED = 1024
SEQ = 512
BATCHES = 4
HEADS = 16
DH = EMBED // HEADS
TOKENS = BATCHES * SEQ
KC = EMBED // P
PAIRS = HEADS // 2
QT = SEQ // P
STEPS = 2 * QT
HALVES = 2
UNITS = PAIRS * BATCHES
UPH = UNITS // HALVES
GROUP_MM = 3 * KC
MM_STEP = 3 * GROUP_MM // STEPS
TILES = TOKENS // P
EXPERTS = 8
RANK = 16
HR = EXPERTS * RANK
LOGITS = EXPERTS
WLT = 256
LN_STEPS = 5
ARW = HR + LOGITS
SCORE_SCALE = float(EXPERTS) * (32.0 / RANK)
EPS = 1e-5
MASKED = -1e30
SOFT = DH ** -0.5
CHUNKS = 8
SWAP = [p ^ 1 for p in range(32)]


def sandwich_kernel(nc, x, wqkv, wo, ar, bt, br, cos, sin, scratch, out):
    with ExitStack() as ctx:
        def sb(stack, name, shape, dt=F32):
            return stack.enter_context(nc.sbuf_tensor(name, shape, dt))

        def sem(name):
            return ctx.enter_context(nc.semaphore(name))

        bank = [ctx.enter_context(nc.psum_tensor(f"bank{i}", [P, 512], F32)) for i in range(8)]
        grp_ps = bank[0:2]
        sc_ps = bank[2:4]
        pt_ps = bank[4:6]
        o_ps = bank[6]
        tr_ps = bank[7]
        y_ps = [grp_ps, sc_ps]

        big_hi = sb(ctx, "big_hi", [P, 8192], F32R)
        big_lo = sb(ctx, "big_lo", [P, 8192], F32R)
        xT_hi = big_hi[:, :].rearrange("p (b c t) -> p b c t", b=2, c=KC)
        xT_lo = big_lo[:, :].rearrange("p (b c t) -> p b c t", b=2, c=KC)
        wo_hi = big_hi[:, :].rearrange("p (c n) -> p c n", c=KC)
        wo_lo = big_lo[:, :].rearrange("p (c n) -> p c n", c=KC)
        w_raw = sb(ctx, "w_raw", [P, 3, EMBED])
        w_hi = sb(ctx, "w_hi", [P, 3, EMBED], F32R)
        w_lo = sb(ctx, "w_lo", [P, 3, EMBED], F32R)
        oT_hi = w_hi[:, 0:2, :].rearrange("p i (c t) -> p i c t", c=KC)
        oT_lo = w_lo[:, 0:2, :].rearrange("p i (c t) -> p i c t", c=KC)
        xin = sb(ctx, "xin", [P, 2, EMBED])
        oT = xin[:, :, :].rearrange("p i (c t) -> p i c t", c=KC)
        ident = sb(ctx, "ident", [P, P])
        stats = sb(ctx, "stats", [P, 2, 6])
        mv = sb(ctx, "mv", [P, 2])
        ve = sb(ctx, "ve", [P, 1])
        lnv = sb(ctx, "lnv", [P, 1])
        r0 = sb(ctx, "r0", [P, 1])
        rr = sb(ctx, "rr", [P, 1])
        cc = sb(ctx, "cc", [P, 1])
        rstd = sb(ctx, "rstd", [P, 1])
        nmr = sb(ctx, "nmr", [P, 1])

        sB = ExitStack()
        qk_hi = sb(sB, "qk_hi", [P, 2, 2, SEQ], F32R)
        qk_lo = sb(sB, "qk_lo", [P, 2, 2, SEQ], F32R)
        v_hl = sb(sB, "v_hl", [P, 2, QT, 2, 2 * DH], F32R)
        mask = sb(sB, "mask", [P, SEQ])
        cos_sb = sb(sB, "cos_sb", [P, SEQ])
        sin_sb = sb(sB, "sin_sb", [P, SEQ])
        raw = sb(sB, "raw", [P, SEQ])
        swapped = sb(sB, "swapped", [P, SEQ])
        rot_c = sb(sB, "rot_c", [P, SEQ])
        rot_s = sb(sB, "rot_s", [P, SEQ])
        vraw = sb(sB, "vraw", [P, SEQ])
        neg = sb(sB, "neg", [P, 2, SEQ])
        prob = sb(sB, "prob", [P, 4, SEQ])
        pT_hi = sb(sB, "pT_hi", [P, 2, QT, SEQ], F32R)
        pT_lo = sb(sB, "pT_lo", [P, 2, QT, SEQ], F32R)
        nmax = sb(sB, "nmax", [P, 4])
        rsum = sb(sB, "rsum", [P, 4])
        rinv = sb(sB, "rinv", [P, 4])
        o_low = sb(sB, "o_low", [DH, SEQ])
        o_sum = sb(sB, "o_sum", [DH, 2, SEQ])
        xn = sb(sB, "xn", [P, 2, EMBED])
        sB.close()

        sC = ExitStack()
        ar_hi = sb(sC, "ar_hi", [P, KC, ARW], F32R)
        ar_lo = sb(sC, "ar_lo", [P, KC, ARW], F32R)
        bt_hi = sb(sC, "bt_hi", [P, EMBED], F32R)
        bt_lo = sb(sC, "bt_lo", [P, EMBED], F32R)
        ar_raw = sb(sC, "ar_raw", [P, KC, ARW])
        bt_raw = sb(sC, "bt_raw", [P, EMBED])
        br_sb = sb(sC, "br_sb", [P, LOGITS])
        xres = sb(sC, "xres", [P, 2, EMBED])
        x1 = sb(sC, "x1", [P, 2, EMBED])
        z = sb(sC, "z", [P, EMBED])
        xn2 = sb(sC, "xn2", [P, EMBED])
        x2T_hi = sb(sC, "x2T_hi", [P, KC, P], F32R)
        x2T_lo = sb(sC, "x2T_lo", [P, KC, P], F32R)
        logit = sb(sC, "logit", [P, LOGITS])
        lmax = sb(sC, "lmax", [P, 1])
        lexp = sb(sC, "lexp", [P, LOGITS])
        lsum = sb(sC, "lsum", [P, 1])
        linv = sb(sC, "linv", [P, 1])
        score = sb(sC, "score", [P, LOGITS])
        wlow = sb(sC, "wlow", [P, HR])
        wlT_hi = sb(sC, "wlT_hi", [P, P], F32R)
        wlT_lo = sb(sC, "wlT_lo", [P, P], F32R)
        res = sb(sC, "res", [P, 2, EMBED])
        sC.close()

        tables_in = sem("tables_in")
        x_in = [sem(f"x_in{i}") for i in range(2)]
        w_in = [sem(f"w_in{m}") for m in range(3)]
        consts = sem("consts")
        ln_stat = sem("ln_stat")
        ln_dve = sem("ln_dve")
        ln_act = sem("ln_act")
        normed = sem("normed")
        tr_done = sem("tr_done")
        tr_hi = sem("tr_hi")
        tr_lo = sem("tr_lo")
        w_hi_done = [sem(f"w_hi_done{m}") for m in range(3)]
        w_lo_done = [sem(f"w_lo_done{m}") for m in range(3)]
        grp_done = sem("grp_done")
        grp_read = sem("grp_read")
        swap_done = sem("swap_done")
        rot_mul = sem("rot_mul")
        rot_done = sem("rot_done")
        qk_hi_done = sem("qk_hi_done")
        qk_lo_done = sem("qk_lo_done")
        s_done = sem("s_done")
        neg_done = sem("neg_done")
        exp_done = sem("exp_done")
        inv_done = sem("inv_done")
        prob_done = sem("prob_done")
        t_done = sem("t_done")
        pt_hi_done = sem("pt_hi_done")
        pt_lo_done = sem("pt_lo_done")
        pv_done = sem("pv_done")
        olow_done = sem("olow_done")
        osum_done = sem("osum_done")
        o_out = [sem(f"o_out{i}") for i in range(2)]
        wo_in = [sem(f"wo_in{i}") for i in range(3)]
        wo_hi_done = sem("wo_hi_done")
        wo_lo_done = sem("wo_lo_done")
        ffn_in = sem("ffn_in")
        ffn_hi_done = sem("ffn_hi_done")
        ffn_lo_done = sem("ffn_lo_done")
        oT_in = [sem(f"oT_in{i}") for i in range(2)]
        xres_in = [sem(f"xres_in{i}") for i in range(2)]
        oT_hi_done = sem("oT_hi_done")
        oT_lo_done = sem("oT_lo_done")
        y_done = sem("y_done")
        x1_done = sem("x1_done")
        x2t_done = sem("x2t_done")
        x2T_hi_done = sem("x2T_hi_done")
        x2T_lo_done = sem("x2T_lo_done")
        low_done = sem("low_done")
        soft_dve = sem("soft_dve")
        soft_exp = sem("soft_exp")
        wlow_done = sem("wlow_done")
        wlt_done = sem("wlt_done")
        wlT_hi_done = sem("wlT_hi_done")
        wlT_lo_done = sem("wlT_lo_done")
        e_done = sem("e_done")
        res_done = sem("res_done")
        out_out = [sem(f"out_out{i}") for i in range(2)]

        gate_dve = sem("gate_dve")
        gate_pool = sem("gate_pool")

        block = ctx.enter_context(nc.Block())

        def late(count, first):
            return not isinstance(count, int) or count >= first

        def real(u):
            return not isinstance(u, int) or 0 <= u < UNITS

        def trailing(u, s, lag):
            at = s - lag
            a, q = u - 1 + at // STEPS, at % STEPS
            return a, q, STEPS * a + q

        def x_fill(batch, c):
            v_before = {0: 0, 1: 0, 2: UPH - 2, 3: UPH - 1}[batch] + (1 if batch >= 2 and c >= 2 else 0)
            return CHUNKS * batch + c + v_before

        def v_fill(u, half):
            chunks = 2 * CHUNKS if half == 0 else 4 * CHUNKS
            if isinstance(u, int):
                chunks = {UPH - 1: 2 * CHUNKS + 2, UPH: 3 * CHUNKS + 2}.get(u, 2 * CHUNKS if u < UPH else 4 * CHUNKS)
            return u - 1 + chunks

        def x_turns(u, s):
            if not isinstance(u, int):
                return 0, [], []
            now = {0: 1, UPH - 1: 2, UPH: 3}.get(u)
            nxt = {UPH - 2: 2, UPH - 1: 3}.get(u)
            tiles = []
            if now is not None and s in (1, 3):
                tiles.append(4 * now + (s + 3) // 2)
            if nxt is not None and s in (5, 7):
                tiles.append(4 * nxt + (s - 5) // 2)
            chunks = [[0], [1], [2, 3], [4], [5], [6], [7], []][s] if now is not None else []
            return now, tiles, chunks

        def run_slots(eng, slot):
            for half in range(HALVES):
                slot(0, 0, half)
                slot(0, 1, half)
                with eng.Fori(1, PAIRS - 1) as pair:
                    slot(pair, 0, half)
                    slot(pair, 1, half)
                slot(PAIRS - 1, 0, half)
                slot(PAIRS - 1, 1, half)
            slot(PAIRS, 0, 1)
            slot(PAIRS, 1, 1)

        def tiled(t):
            return not isinstance(t, int) or 0 <= t < TILES

        def ln_first(t):
            return TILES + 3 * t - (1 if late(t, 1) else 0)

        def ln_second(t):
            return ln_first(t) + 1

        def ln_third(t):
            return TILES + 3 * t + 4 if not (isinstance(t, int) and t == TILES - 1) else 4 * TILES - 1

        @block.sync
        def _(sp):
            def load_x(n):
                if n >= 2:
                    sp.wait_ge(normed, n - 1)
                sp.dma_start(xin[:, n % 2, :], x[n * P:(n + 1) * P, :]).then_inc(x_in[n % 2], 16)

            def load_w(m, n, pair):
                if late(n, 1):
                    sp.wait_ge(w_hi_done[m], n)
                    sp.wait_ge(w_lo_done[m], n)
                sp.dma_start(w_raw[:, m, :], wqkv[m, pair, :, :]).then_inc(w_in[m], 16)

            def store_o(u, pair, b, half, h):
                if real(u):
                    sp.wait_ge(osum_done, 2 * u + h + 1)
                    batch = 2 * half + b
                    sp.dma_start(scratch[2 * pair + h, :, batch * SEQ:(batch + 1) * SEQ],
                                 o_sum[:, h, :]).then_inc(o_out[h], 16)

            load_x(0)
            load_w(0, 0, 0)
            load_x(1)
            sp.dma_start(cos_sb[:, :], cos).then_inc(tables_in, 16)
            sp.dma_start(sin_sb[:, :], sin).then_inc(tables_in, 16)
            load_w(1, 0, 0)
            load_w(2, 0, 0)
            for n in range(2, 6):
                load_x(n)

            def slot(pair, b, half):
                u = 2 * pair + b + UPH * half
                crossing = isinstance(pair, int) and pair == 0
                stored = (PAIRS - 1, half - 1) if crossing else (pair - 1, half)
                more = b == 0 and not (isinstance(u, int) and u >= UNITS - 2)
                n = pair + PAIRS * half + 1
                nxt = (pair + 1) % PAIRS if isinstance(pair, int) else pair + 1
                if more:
                    load_w(0, n, nxt)
                    load_w(1, n, nxt)
                store_o(u - 2, stored[0], b, stored[1], 0)
                early = {0: (6, 7), UPH - 2: (8, 9), UPH - 1: (10, 11), UPH: (14, 15)}
                for t in early.get(u, ()) if isinstance(u, int) else ():
                    load_x(t)
                if more:
                    load_w(2, n, nxt)
                store_o(u - 2, stored[0], b, stored[1], 1)
                if isinstance(u, int) and u == UPH - 1:
                    load_x(12)
                    load_x(13)

            run_slots(sp, slot)

            for c in range(KC):
                if c < 3:
                    sp.wait_ge(w_hi_done[c], 2 * PAIRS)
                    sp.wait_ge(w_lo_done[c], 2 * PAIRS)
                else:
                    sp.wait_ge(wo_hi_done, c - 2)
                    sp.wait_ge(wo_lo_done, c - 2)
                sp.dma_start(w_raw[:, c % 3, :], wo[c * P:(c + 1) * P, :]).then_inc(wo_in[c % 3], 16)
            sp.wait_ge(pv_done, HEADS * BATCHES)
            for h in range(2):
                sp.wait_ge(o_out[h], 16 * UNITS)

            def load_tile(t, i):
                if late(t, 2):
                    sp.wait_ge(oT_hi_done, t - 1)
                    sp.wait_ge(oT_lo_done, t - 1)
                sp.dma_start(oT[:, i, :, :],
                             scratch.rearrange("(c h) d t -> (h d) c t", h=2)[:, :, bass.ds(t * P, P)]
                             ).then_inc(oT_in[i], 16)
                if late(t, 2):
                    sp.wait_ge(x1_done, t - 1)
                sp.dma_start(xres[:, i, :], x[bass.ds(t * P, P), :]).then_inc(xres_in[i], 16)

            load_tile(0, 0)
            sp.dma_start(ar_raw[:, :, :], ar).then_inc(ffn_in, 16)
            sp.dma_start(bt_raw[:, :], bt).then_inc(ffn_in, 16)
            sp.dma_start(br_sb[:, :], br).then_inc(ffn_in, 16)

            def turn(t, i):
                if tiled(t + 1) and not (isinstance(t, int) and t == TILES):
                    load_tile(t + 1, 1 - i)
                if tiled(t - 2):
                    sp.wait_ge(res_done, t - 1)
                    sp.dma_start(out[bass.ds((t - 2) * P, P), :], res[:, i, :]).then_inc(out_out[i], 16)

            turn(0, 0)
            turn(1, 1)
            with sp.Fori(2, TILES - 2, 2) as t:
                turn(t, 0)
                turn(t + 1, 1)
            for t in range(TILES - 2, TILES + 2):
                turn(t, t % 2)
            sp.wait_ge(out_out[0], 16 * TILES // 2)
            sp.wait_ge(out_out[1], 16 * TILES // 2)

        @block.gpsimd
        def _(pool):
            pool.memset(ident[:, :], 0.0).then_inc(consts, 1)
            pool.memset(mask[:, :], 0.0).then_inc(consts, 1)
            pool.wait_ge(consts, 2)
            pool.affine_select(out=ident[:, :], in_=ident[:, :], compare_op=ALU.not_equal, fill=1.0,
                               base=0, pattern=[[-1, P]], channel_multiplier=1).then_inc(consts, 1)
            diag = mask[:, SEQ - P:SEQ]
            pool.affine_select(out=diag, in_=diag, compare_op=ALU.is_ge, fill=MASKED,
                               base=0, pattern=[[-1, P]], channel_multiplier=1).then_inc(consts, 1)
            pool.wait_ge(tables_in, 32)

            def divide(u, s):
                a, q, g = trailing(u, s, 1)
                if real(a):
                    pool.wait_ge(inv_done, g + 1)
                    pool.sem_inc(gate_pool, 1)
                    p = prob[:, q % 4, 0:P * (q % QT + 1)]
                    pool.tensor_scalar(p, p, rinv[:, q % 4:q % 4 + 1], 1.0, ALU.mult, ALU.mult
                                       ).then_inc(prob_done, 1)

            def rotate(u, k):
                m = 2 * u + k
                pool.wait_ge(grp_read, 3 * u + k + 1)
                if late(m, 1):
                    pool.wait_ge(rot_done, m)
                    pool.wait_ge(qk_hi_done, m)
                    pool.wait_ge(qk_lo_done, m)
                pool.tensor_tensor(rot_c[:, :], raw[:, :], cos_sb[:, :], ALU.mult).then_inc(rot_mul, 1)
                pool.wait_ge(swap_done, m + 1)
                pool.tensor_tensor(rot_s[:, :], swapped[:, :], sin_sb[:, :], ALU.mult).then_inc(rot_mul, 1)

            def slot(pair, b, half):
                u = 2 * pair + b + UPH * half
                for s in range(STEPS):
                    divide(u, s)
                    if real(u) and s in (3, 6):
                        rotate(u, s // 6)

            run_slots(pool, slot)

        @block.scalar
        def _(act):
            def ln_rstd(n):
                act.wait_ge(ln_dve, LN_STEPS * n + 1)
                act.activation(lnv[:, :], ve[:, :], ACT.Ln).then_inc(ln_act, 1)
                act.wait_ge(ln_act, 2 * n + 1)
                act.activation(r0[:, :], lnv[:, :], ACT.Exp, scale=-0.5).then_inc(ln_act, 1)
                act.wait_ge(ln_dve, LN_STEPS * n + LN_STEPS)

            def normal(dst, src):
                return act.activation(dst, src, ACT.Identity, bias=nmr[:, 0:1], scale=rstd[:, 0:1])

            def x_tile(n):
                ln_rstd(n)
                if n >= 2:
                    act.wait_ge(tr_done, x_fill((n - 2) // 4, 2 * ((n - 2) % 4) + 1) + 1)
                normal(xn[:, n % 2, :], xin[:, n % 2, :]).then_inc(normed, 1)

            def x_chunk(batch, c):
                act.wait_ge(tr_done, x_fill(batch, c) + 1)
                if batch >= 2 and c == 0:
                    act.wait_ge(grp_done, 3 * (UPH - 3 + batch))
                dst = xT_hi[:, batch % 2, 4 * (c % 2):4 * (c % 2) + 4, P * (c // 2):P * (c // 2) + P]
                act.activation(dst, tr_ps[:, :].rearrange("p (c t) -> p c t", c=4), ACT.Copy).then_inc(tr_hi, 1)

            def w_high(m, n):
                act.wait_ge(w_in[m], 16 * n + 16)
                if late(n, 1):
                    act.wait_ge(grp_done, 6 * n - 2 + m)
                act.activation(w_hi[:, m, :], w_raw[:, m, :], ACT.Copy).then_inc(w_hi_done[m], 1)

            def exponent(u, s):
                a, q, g = trailing(u, s, 1)
                if real(a):
                    n = P * (q % QT + 1)
                    act.wait_ge(neg_done, g + 1)
                    if late(g, 4):
                        act.wait_ge(t_done, g - 3)
                    act.activation(prob[:, q % 4, 0:n], neg[:, q % 2, 0:n], ACT.Exp, scale=-1.0,
                                   bias=nmax[:, q % 4:q % 4 + 1], accum_out=rsum[:, q % 4:q % 4 + 1]
                                   ).then_inc(exp_done, 1)

            def pt_high(u, s):
                a, q, g = trailing(u, s, 3)
                if real(a):
                    i, h = q % QT, q // QT
                    act.wait_ge(t_done, g + 1)
                    if late(a, 1):
                        act.wait_ge(pv_done, 2 * a + h - 1)
                    act.activation(pT_hi[:, h, 0:i + 1, P * i:P * i + P],
                                   pt_ps[q % 2][:, 0:P * (i + 1)].rearrange("p (j t) -> p j t", j=i + 1),
                                   ACT.Copy).then_inc(pt_hi_done, 1)

            def qk_raw(u, b, k):
                m = 2 * u + k
                act.wait_ge(grp_done, 3 * u + k + 1)
                if late(m, 1):
                    act.wait_ge(rot_done, m)
                act.activation(raw[:, :], grp_ps[(b + k) % 2][:, :], ACT.Copy).then_inc(grp_read, 1)

            def qk_high(u, b, k):
                act.wait_ge(rot_done, 2 * u + k + 1)
                if late(u, 2):
                    act.wait_ge(s_done, STEPS * (u - 1))
                act.activation(qk_hi[:, b, k, :], rot_c[:, :], ACT.Copy).then_inc(qk_hi_done, 1)

            def v_raw(u, b, fill):
                act.wait_ge(grp_done, 3 * u + 3)
                act.wait_ge(tr_done, fill)
                act.activation(vraw[:, :], grp_ps[b][:, :], ACT.Copy).then_inc(grp_read, 1)

            def v_high(u, b, fill):
                act.wait_ge(tr_done, fill + 1)
                if late(u, 2):
                    act.wait_ge(pv_done, 2 * (u - 1))
                act.activation(v_hl[:, b, :, :, 0:DH].rearrange("p j h d -> p (j h) d"),
                               tr_ps[:, :].rearrange("p (j d) -> p j d", d=DH), ACT.Copy).then_inc(tr_hi, 1)

            def o_lower(a, h):
                n = 2 * a + h
                act.wait_ge(pv_done, n + 1)
                if late(n, 1):
                    act.wait_ge(osum_done, n)
                act.activation(o_low[:, :], o_ps[DH:2 * DH, :], ACT.Copy).then_inc(olow_done, 1)

            def slot(pair, b, half):
                u = 2 * pair + b + UPH * half
                n = pair + PAIRS * half
                fill = v_fill(u, half)
                for s in range(STEPS):
                    exponent(u, s)
                    if s == 0 and real(u - 1):
                        v_raw(u - 1, 1 - b, v_fill(u - 1, half) + 1)
                    if s == 1 and real(u - 2):
                        o_lower(u - 2, 0)
                    if s == 5 and real(u - 2):
                        o_lower(u - 2, 1)
                    if s == 2 and real(u - 1):
                        v_high(u - 1, 1 - b, fill)
                    pt_high(u, s)
                    if real(u):
                        if s == 2 and b == 0 and late(n, 1):
                            w_high(2, n)
                        if s == 3:
                            qk_raw(u, b, 0)
                        if s == 4:
                            qk_high(u, b, 0)
                        if s == 5:
                            qk_raw(u, b, 1)
                        if s == 7:
                            qk_high(u, b, 1)
                        if b == 1 and not (isinstance(u, int) and u == UNITS - 1):
                            if s == 4:
                                w_high(0, n + 1)
                            if s == 7:
                                w_high(1, n + 1)
                    batch, tiles, chunks = x_turns(u, s)
                    for c in chunks:
                        x_chunk(batch, c)
                    for t in tiles:
                        x_tile(t)

            act.preload_act_table_set("natural_log_exp_and_others")
            x_tile(0)
            w_high(0, 0)
            for n in range(4):
                x_tile(n + 1)
                x_chunk(0, 2 * n)
                x_chunk(0, 2 * n + 1)
                if n < 2:
                    w_high(n + 1, 0)
            x_tile(5)
            run_slots(act, slot)

            act.wait_ge(grp_done, 3 * UNITS)
            for c in range(KC):
                act.wait_ge(wo_in[c % 3], 16 * (c // 3 + 1))
                act.activation(wo_hi[:, c, :], w_raw[:, c % 3, :], ACT.Copy).then_inc(wo_hi_done, 1)
            act.wait_ge(pv_done, HEADS * BATCHES)
            act.wait_ge(osum_done, HEADS * BATCHES)

            def oT_high(t, i, count):
                act.wait_ge(oT_in[i], count)
                if late(t, 2):
                    act.wait_ge(y_done, t - 1)
                act.activation(oT_hi[:, i, :, :], oT[:, i, :, :], ACT.Copy).then_inc(oT_hi_done, 1)

            oT_high(0, 0, 16)
            act.wait_ge(ffn_in, 48)
            act.activation(ar_hi[:, :, :], ar_raw[:, :, :], ACT.Copy).then_inc(ffn_hi_done, 1)
            act.activation(bt_hi[:, :], bt_raw[:, :], ACT.Copy).then_inc(ffn_hi_done, 1)

            def turn(t, i):
                if tiled(t - 1) and not (isinstance(t, int) and t > TILES):
                    ln_rstd(ln_first(t - 1))
                    if late(t, 3):
                        act.wait_ge(res_done, t - 2)
                    for k in range(2):
                        done = normal(z[:, 512 * k:512 * k + 512], y_ps[1 - i][k][:, :])
                    done.then_inc(normed, 1)
                if tiled(t - 2):
                    act.wait_ge(wlt_done, t - 1)
                    if late(t, 3):
                        act.wait_ge(e_done, t - 2)
                    act.activation(wlT_hi[:, :], o_ps[:, WLT:WLT + P], ACT.Copy).then_inc(wlT_hi_done, 1)
                if tiled(t - 1) and not (isinstance(t, int) and t > TILES):
                    ln_rstd(ln_second(t - 1))
                    if late(t, 2):
                        act.wait_ge(x2t_done, 2 * (t - 1))
                    normal(xn2[:, :], x1[:, 1 - i, :]).then_inc(normed, 1)
                if tiled(t - 2):
                    ln_rstd(ln_third(t - 2))
                    for k in range(2):
                        done = normal(z[:, 512 * k:512 * k + 512], pt_ps[k][:, :])
                    done.then_inc(normed, 1)
                if tiled(t + 1) and not (isinstance(t, int) and t >= TILES - 1):
                    oT_high(t + 1, 1 - i, 8 * (t + 1 - (1 - i)) + 16)
                if tiled(t - 1) and not (isinstance(t, int) and t > TILES):
                    for k in range(2):
                        act.wait_ge(x2t_done, 2 * (t - 1) + k + 1)
                        if late(t, 2) and k == 0:
                            act.wait_ge(low_done, t - 1)
                        act.activation(x2T_hi[:, 4 * k:4 * k + 4, :],
                                       tr_ps[:, :].rearrange("p (c t) -> p c t", c=4),
                                       ACT.Copy).then_inc(x2T_hi_done, 1)
                    act.wait_ge(soft_dve, 5 * (t - 1) + 2)
                    act.activation(lexp[:, :], logit[:, :], ACT.Exp, bias=lmax[:, 0:1],
                                   accum_out=lsum[:, 0:1]).then_inc(soft_exp, 1)

            turn(0, 0)
            turn(1, 1)
            turn(2, 0)
            turn(3, 1)
            with act.Fori(4, TILES - 2, 2) as t:
                turn(t, 0)
                turn(t + 1, 1)
            for t in range(TILES - 2, TILES + 2):
                turn(t, t % 2)

        @block.vector
        def _(dve):
            def layernorm(n, src):
                dve.bn_stats(stats[:, 0, :], src[0]).then_inc(ln_stat, 1)
                dve.bn_stats(stats[:, 1, :], src[1]).then_inc(ln_stat, 1)
                dve.wait_ge(ln_stat, 3 * n + 2)
                dve.sem_inc(gate_dve, 1)
                dve.bn_aggr(mv[:, :], stats[:, :, :].rearrange("p a b -> p (a b)")).then_inc(ln_stat, 1)
                dve.wait_ge(ln_stat, 3 * n + 3)
                dve.tensor_scalar(ve[:, :], mv[:, 1:2], EPS, None, ALU.add).then_inc(ln_dve, 1)
                dve.wait_ge(ln_act, 2 * n + 2)
                dve.wait_ge(ln_dve, LN_STEPS * n + 1)
                dve.scalar_tensor_tensor(out=rr[:, :], in0=r0[:, :], scalar=ve[:, 0:1], in1=r0[:, :],
                                         op0=ALU.mult, op1=ALU.mult).then_inc(ln_dve, 1)
                dve.wait_ge(ln_dve, LN_STEPS * n + 2)
                dve.tensor_scalar(cc[:, :], rr[:, :], -0.5, 1.5, ALU.mult, ALU.add).then_inc(ln_dve, 1)
                if late(n, 1):
                    dve.wait_ge(normed, n)
                dve.wait_ge(ln_dve, LN_STEPS * n + 3)
                dve.tensor_tensor(rstd[:, :], cc[:, :], r0[:, :], ALU.mult).then_inc(ln_dve, 1)
                dve.wait_ge(ln_dve, LN_STEPS * n + 4)
                dve.scalar_tensor_tensor(out=nmr[:, :], in0=mv[:, 0:1], scalar=-1.0, in1=rstd[:, :],
                                         op0=ALU.mult, op1=ALU.mult).then_inc(ln_dve, 1)

            def x_tile(n):
                dve.wait_ge(x_in[n % 2], 16 * (n // 2 + 1))
                layernorm(n, [xin[:, n % 2, 0:512], xin[:, n % 2, 512:1024]])

            def x_chunk(batch, c):
                dve.wait_ge(tr_hi, x_fill(batch, c) + 1)
                at = (slice(None), batch % 2, slice(4 * (c % 2), 4 * (c % 2) + 4),
                      slice(P * (c // 2), P * (c // 2) + P))
                dve.tensor_tensor(xT_lo[at], tr_ps[:, :].rearrange("p (c t) -> p c t", c=4),
                                  xT_hi[at].bitcast(F32), ALU.subtract).then_inc(tr_lo, 1)

            def w_low(m, n):
                dve.wait_ge(w_hi_done[m], n + 1)
                dve.tensor_tensor(w_lo[:, m, :], w_raw[:, m, :], w_hi[:, m, :].bitcast(F32), ALU.subtract
                                  ).then_inc(w_lo_done[m], 1)

            def negate(u, s):
                a, q, g = trailing(u, s, 1)
                if real(a):
                    n = P * (q % QT + 1)
                    dve.wait_ge(s_done, g + 1)
                    if late(g, 2):
                        dve.wait_ge(exp_done, g - 1)
                    dve.sem_inc(gate_dve, 1)
                    dve.tensor_tensor_reduce(neg[:, q % 2, 0:n], sc_ps[q % 2][:, 0:n], mask[:, SEQ - n:SEQ],
                                             -SOFT, 3e38, ALU.add, ALU.min, nmax[:, q % 4:q % 4 + 1]
                                             ).then_inc(neg_done, 1)

            def invert(u, s):
                a, q, g = trailing(u, s, 1)
                if real(a):
                    dve.wait_ge(exp_done, g + 1)
                    if late(g, 4):
                        dve.wait_ge(prob_done, g - 3)
                    dve.reciprocal(rinv[:, q % 4:q % 4 + 1], rsum[:, q % 4:q % 4 + 1]).then_inc(inv_done, 1)

            def pt_low(u, s):
                a, q, g = trailing(u, s, 3)
                if real(a):
                    i, h = q % QT, q // QT
                    dve.wait_ge(pt_hi_done, g + 1)
                    at = (slice(None), h, slice(0, i + 1), slice(P * i, P * i + P))
                    dve.tensor_tensor(pT_lo[at], pt_ps[q % 2][:, 0:P * (i + 1)].rearrange("p (j t) -> p j t", j=i + 1),
                                      pT_hi[at].bitcast(F32), ALU.subtract).then_inc(pt_lo_done, 1)

            def swap(u, k):
                m = 2 * u + k
                dve.wait_ge(grp_read, 3 * u + k + 1)
                if late(m, 1):
                    dve.wait_ge(rot_mul, 2 * m)
                dve.sem_inc(gate_dve, 1)
                dve.stream_shuffle(swapped[:, :], raw[:, :], SWAP).then_inc(swap_done, 1)

            def rotate(u, k):
                m = 2 * u + k
                dve.wait_ge(rot_mul, 2 * m + 2)
                dve.tensor_tensor(rot_c[:, :], rot_c[:, :], rot_s[:, :], ALU.add).then_inc(rot_done, 1)

            def qk_low(u, b, k):
                dve.wait_ge(qk_hi_done, 2 * u + k + 1)
                dve.tensor_tensor(qk_lo[:, b, k, :], rot_c[:, :], qk_hi[:, b, k, :].bitcast(F32), ALU.subtract
                                  ).then_inc(qk_lo_done, 1)

            def v_low(b, fill):
                dve.wait_ge(tr_hi, fill + 1)
                dve.tensor_tensor(v_hl[:, b, :, :, DH:2 * DH].rearrange("p j h d -> p (j h) d"),
                                  tr_ps[:, :].rearrange("p (j d) -> p j d", d=DH),
                                  v_hl[:, b, :, :, 0:DH].rearrange("p j h d -> p (j h) d").bitcast(F32),
                                  ALU.subtract).then_inc(tr_lo, 1)

            def o_add(a, h):
                dve.wait_ge(olow_done, 2 * a + h + 1)
                if late(a, 1):
                    dve.wait_ge(o_out[h], 16 * a)
                dve.tensor_tensor(o_sum[:, h, :], o_ps[0:DH, :], o_low[:, :], ALU.add).then_inc(osum_done, 1)

            def slot(pair, b, half):
                u = 2 * pair + b + UPH * half
                n = pair + PAIRS * half
                fill = v_fill(u, half)
                for s in range(STEPS):
                    negate(u, s)
                    if s == 0 and real(u - 1):
                        qk_low(u - 1, 1 - b, 1)
                    if s == 1 and real(u - 2):
                        o_add(u - 2, 0)
                    if s == 5 and real(u - 2):
                        o_add(u - 2, 1)
                    if real(u):
                        if s == 3:
                            swap(u, 0)
                        if s == 4:
                            rotate(u, 0)
                        if s == 6:
                            swap(u, 1)
                        if s == 7:
                            rotate(u, 1)
                    invert(u, s)
                    if s == 2 and real(u - 1):
                        v_low(1 - b, fill)
                    pt_low(u, s)
                    if real(u):
                        if s == 3 and b == 0 and late(n, 1):
                            w_low(2, n)
                        if s == 4:
                            qk_low(u, b, 0)
                        if b == 1 and not (isinstance(u, int) and u == UNITS - 1):
                            if s == 5:
                                w_low(0, n + 1)
                            if s == 7:
                                w_low(1, n + 1)
                    batch, tiles, chunks = x_turns(u, s)
                    for c in chunks:
                        x_chunk(batch, c)
                    for t in tiles:
                        x_tile(t)

            dve.wait_ge(consts, 4)
            x_tile(0)
            w_low(0, 0)
            for n in range(4):
                x_tile(n + 1)
                x_chunk(0, 2 * n)
                x_chunk(0, 2 * n + 1)
                if n < 2:
                    w_low(n + 1, 0)
            x_tile(5)
            run_slots(dve, slot)

            for c in range(KC):
                dve.wait_ge(wo_hi_done, c + 1)
                dve.tensor_tensor(wo_lo[:, c, :], w_raw[:, c % 3, :], wo_hi[:, c, :].bitcast(F32), ALU.subtract
                                  ).then_inc(wo_lo_done, 1)
            dve.wait_ge(pv_done, HEADS * BATCHES)
            for h in range(2):
                dve.wait_ge(o_out[h], 16 * UNITS)

            def oT_low(t, i):
                dve.wait_ge(oT_hi_done, t + 1)
                dve.tensor_tensor(oT_lo[:, i, :, :], oT[:, i, :, :], oT_hi[:, i, :, :].bitcast(F32), ALU.subtract
                                  ).then_inc(oT_lo_done, 1)

            oT_low(0, 0)
            dve.wait_ge(ffn_hi_done, 2)
            dve.tensor_tensor(ar_lo[:, :, :], ar_raw[:, :, :], ar_hi[:, :, :].bitcast(F32), ALU.subtract
                              ).then_inc(ffn_lo_done, 1)
            dve.tensor_tensor(bt_lo[:, :], bt_raw[:, :], bt_hi[:, :].bitcast(F32), ALU.subtract
                              ).then_inc(ffn_lo_done, 1)

            def turn(t, i):
                middle = tiled(t - 1) and not (isinstance(t, int) and t > TILES)
                if middle:
                    dve.wait_ge(y_done, t)
                    layernorm(ln_first(t - 1), [y[:, :] for y in y_ps[1 - i]])
                if tiled(t - 2):
                    dve.wait_ge(wlT_hi_done, t - 1)
                    dve.tensor_tensor(wlT_lo[:, :], o_ps[:, WLT:WLT + P], wlT_hi[:, :].bitcast(F32), ALU.subtract
                                      ).then_inc(wlT_lo_done, 1)
                if middle:
                    dve.wait_ge(normed, ln_first(t - 1) + 1)
                    dve.wait_ge(xres_in[1 - i], 8 * (t - 1 - (1 - i)) + 16)
                    dve.tensor_tensor(x1[:, 1 - i, :], z[:, :], xres[:, 1 - i, :], ALU.add).then_inc(x1_done, 1)
                    dve.wait_ge(x1_done, t)
                    layernorm(ln_second(t - 1), [x1[:, 1 - i, 0:512], x1[:, 1 - i, 512:1024]])
                if tiled(t - 2):
                    dve.wait_ge(e_done, t - 1)
                    layernorm(ln_third(t - 2), [e[:, :] for e in pt_ps])
                    dve.wait_ge(normed, ln_third(t - 2) + 1)
                    if late(t, 4):
                        dve.wait_ge(out_out[i], 8 * (t - i) - 16)
                    dve.tensor_tensor(res[:, i, :], z[:, :], x1[:, i, :], ALU.add).then_inc(res_done, 1)
                if tiled(t + 1) and not (isinstance(t, int) and t >= TILES - 1):
                    oT_low(t + 1, 1 - i)
                if middle:
                    for k in range(2):
                        dve.wait_ge(x2T_hi_done, 2 * (t - 1) + k + 1)
                        dve.tensor_tensor(x2T_lo[:, 4 * k:4 * k + 4, :],
                                          tr_ps[:, :].rearrange("p (c t) -> p c t", c=4),
                                          x2T_hi[:, 4 * k:4 * k + 4, :].bitcast(F32), ALU.subtract
                                          ).then_inc(x2T_lo_done, 1)
                    m = 5 * (t - 1)
                    dve.wait_ge(low_done, t)
                    dve.tensor_tensor(logit[:, :], o_ps[:, HR:ARW], br_sb[:, :], ALU.add).then_inc(soft_dve, 1)
                    dve.wait_ge(soft_dve, m + 1)
                    dve.tensor_reduce(lmax[:, :], logit[:, :], AX.X, ALU.max, negate=True).then_inc(soft_dve, 1)
                    dve.wait_ge(soft_exp, t)
                    dve.reciprocal(linv[:, :], lsum[:, :]).then_inc(soft_dve, 1)
                    dve.wait_ge(soft_dve, m + 3)
                    dve.tensor_scalar(score[:, :], lexp[:, :], linv[:, 0:1], SCORE_SCALE, ALU.mult, ALU.mult
                                      ).then_inc(soft_dve, 2)
                    dve.wait_ge(soft_dve, m + 5)
                    if late(t, 2):
                        dve.wait_ge(wlt_done, t - 1)
                    dve.tensor_tensor(wlow[:, :].rearrange("p (h r) -> p h r", h=EXPERTS),
                                      o_ps[:, 0:HR].rearrange("p (h r) -> p h r", h=EXPERTS),
                                      score[:, :].rearrange("p (h o) -> p h o", o=1).to_broadcast([P, EXPERTS, RANK]),
                                      ALU.mult).then_inc(wlow_done, 1)

            turn(0, 0)
            turn(1, 1)
            turn(2, 0)
            turn(3, 1)
            with dve.Fori(4, TILES - 2, 2) as t:
                turn(t, 0)
                turn(t + 1, 1)
            for t in range(TILES - 2, TILES + 2):
                turn(t, t % 2)

        @block.tensor
        def _(pe):
            def products(dst, terms, first, last):
                for n, (lhsT, rhs) in enumerate(terms):
                    mm = pe.matmul(dst, lhsT, rhs, start=first and n == 0, stop=last and n == len(terms) - 1)
                return mm

            def x_chunk(batch, c):
                f = x_fill(batch, c)
                pe.wait_ge(normed, 4 * batch + c // 2 + 1)
                if f:
                    pe.wait_ge(tr_hi, f)
                    pe.wait_ge(tr_lo, f)
                for k in range(4):
                    col = P * (4 * (c % 2) + k)
                    last = pe.transpose(tr_ps[:, P * k:P * k + P], xn[:, c // 2 % 2, col:col + P], ident[:, :])
                last.then_inc(tr_done, 1)

            def v_turn(u, fill):
                pe.wait_ge(grp_read, 3 * u + 3)
                pe.wait_ge(tr_hi, fill)
                pe.wait_ge(tr_lo, fill)
                for k in range(QT):
                    last = pe.transpose(tr_ps[:, P * k:P * k + P], vraw[:, P * k:P * k + P], ident[:, :])
                last.then_inc(tr_done, 1)

            def project(u, b, n, half, first, count):
                for mm in range(first, first + count):
                    k, at = mm // GROUP_MM, mm % GROUP_MM
                    c, part = at // 3, at % 3
                    if at == 0:
                        pe.wait_ge(w_hi_done[k], n + 1)
                        pe.wait_ge(w_lo_done[k], n + 1)
                        if late(3 * u + k, 2):
                            pe.wait_ge(grp_read, 3 * u + k - 1)
                        if isinstance(u, int) and u in (0, 1, UPH, UPH + 1) and k == 0:
                            f = x_fill(2 * half + b, CHUNKS - 1) + 1
                            pe.wait_ge(tr_hi, f)
                            pe.wait_ge(tr_lo, f)
                    w = (w_lo if part == 2 else w_hi)[:, k, P * c:P * c + P]
                    xt = (xT_lo if part == 1 else xT_hi)[:, b, c, :]
                    done = pe.matmul(grp_ps[(b + k) % 2][:, :], w, xt, start=at == 0, stop=at == GROUP_MM - 1)
                    if at == GROUP_MM - 1:
                        done.then_inc(grp_done, 1)

            def scores(u, s, b):
                a, q, g = trailing(u, s, 1)
                if real(a):
                    ab = (b + 1 + (s - 1) // STEPS) % 2
                    i, h = q % QT, q // QT
                    if q == 0:
                        pe.wait_ge(qk_lo_done, 2 * a + 2)
                        pe.wait_ge(qk_hi_done, 2 * a + 2)
                    if late(g, 2):
                        pe.wait_ge(neg_done, g - 1)
                    rows = slice(DH * h, DH * h + DH)
                    qc, kc = slice(P * i, P * i + P), slice(0, P * i + P)
                    q_hi, q_lo = qk_hi[rows, ab, 0, qc], qk_lo[rows, ab, 0, qc]
                    k_hi, k_lo = qk_hi[rows, ab, 1, kc], qk_lo[rows, ab, 1, kc]
                    products(sc_ps[q % 2][:, kc], [(q_hi, k_hi), (q_hi, k_lo), (q_lo, k_hi)], True, True
                             ).then_inc(s_done, 1)

            def turn_probs(u, s):
                a, q, g = trailing(u, s, 3)
                if real(a):
                    pe.wait_ge(prob_done, g + 1)
                    if late(g, 2):
                        pe.wait_ge(pt_hi_done, g - 1)
                        pe.wait_ge(pt_lo_done, g - 1)
                    for j in range(q % QT + 1):
                        last = pe.transpose(pt_ps[q % 2][:, P * j:P * j + P], prob[:, q % 4, P * j:P * j + P],
                                            ident[:, :])
                    last.then_inc(t_done, 1)

            def attend(a, b, h, fill):
                if real(a):
                    g = STEPS * a + QT * h + QT - 1
                    pe.wait_ge(pt_hi_done, g + 1)
                    pe.wait_ge(pt_lo_done, g + 1)
                    if h == 0:
                        pe.wait_ge(tr_hi, fill)
                        pe.wait_ge(tr_lo, fill)
                    if late(2 * a + h, 1):
                        pe.wait_ge(osum_done, 2 * a + h)
                    for j in range(QT):
                        cols = slice(P * j, SEQ)
                        v = v_hl[:, b, j, h, :]
                        last = products(o_ps[:, cols], [(v, pT_hi[:, h, j, cols]), (v, pT_lo[:, h, j, cols])],
                                        j == 0, j == QT - 1)
                    last.then_inc(pv_done, 1)

            def slot(pair, b, half):
                u = 2 * pair + b + UPH * half
                n = pair + PAIRS * half
                fill = v_fill(u, half)
                for s in range(STEPS):
                    third = MM_STEP // 3

                    def project_third(k):
                        if real(u):
                            project(u, b, n, half, MM_STEP * s + third * k, third)

                    project_third(0)
                    if s == 2 and real(u - 1):
                        v_turn(u - 1, fill)
                    scores(u, s, b)
                    project_third(1)
                    turn_probs(u, s)
                    project_third(2)
                    if s == 0:
                        attend(u - 2, b, 0, v_fill(u - 1, half) + 1)
                    if s == 4:
                        attend(u - 2, b, 1, None)
                    batch, _, chunks = x_turns(u, s)
                    for c in chunks:
                        x_chunk(batch, c)

            pe.wait_ge(consts, 4)
            for c in range(CHUNKS):
                x_chunk(0, c)
            run_slots(pe, slot)

            def y_half(t, i, k, c0, c1):
                if k == 0 and c0 == 0:
                    pe.wait_ge(oT_hi_done, t + 1)
                    pe.wait_ge(oT_lo_done, t + 1)
                    if late(t, 2):
                        pe.wait_ge(normed, ln_first(t - 2) + 1)
                for c in range(c0, c1):
                    if isinstance(t, int) and t == 0 and k == 0:
                        pe.wait_ge(wo_hi_done, c + 1)
                        pe.wait_ge(wo_lo_done, c + 1)
                    cols = slice(512 * k, 512 * k + 512)
                    last = products(y_ps[i][k][:, :], [(oT_hi[:, i, c, :], wo_hi[:, c, cols]),
                                                       (oT_lo[:, i, c, :], wo_hi[:, c, cols]),
                                                       (oT_hi[:, i, c, :], wo_lo[:, c, cols])], c == 0, c == KC - 1)
                if k == 1 and c1 == KC:
                    last.then_inc(y_done, 1)

            def x2_turn(t, k):
                if k == 0:
                    pe.wait_ge(normed, ln_second(t) + 1)
                if late(2 * t + k, 1):
                    pe.wait_ge(x2T_hi_done, 2 * t + k)
                    pe.wait_ge(x2T_lo_done, 2 * t + k)
                for c in range(4):
                    last = pe.transpose(tr_ps[:, P * c:P * c + P], xn2[:, P * (4 * k + c):P * (4 * k + c) + P],
                                        ident[:, :])
                last.then_inc(x2t_done, 1)

            def low_rank(t):
                if isinstance(t, int) and t == 0:
                    pe.wait_ge(ffn_lo_done, 2)
                if late(t, 1):
                    pe.wait_ge(wlT_hi_done, t)
                    pe.wait_ge(wlT_lo_done, t)
                for c in range(KC):
                    if c % 4 == 0:
                        pe.wait_ge(x2T_hi_done, 2 * t + c // 4 + 1)
                        pe.wait_ge(x2T_lo_done, 2 * t + c // 4 + 1)
                    last = products(o_ps[:, 0:ARW], [(x2T_hi[:, c, :], ar_hi[:, c, :]), (x2T_lo[:, c, :], ar_hi[:, c, :]),
                                                     (x2T_hi[:, c, :], ar_lo[:, c, :])], c == 0, c == KC - 1)
                last.then_inc(low_done, 1)

            def experts(t):
                pe.wait_ge(wlT_hi_done, t + 1)
                pe.wait_ge(wlT_lo_done, t + 1)
                if late(t, 1):
                    pe.wait_ge(normed, ln_third(t - 1) + 1)
                for k in range(2):
                    cols = slice(512 * k, 512 * k + 512)
                    last = products(pt_ps[k][:, :], [(wlT_hi[:, :], bt_hi[:, cols]), (wlT_lo[:, :], bt_hi[:, cols]),
                                                     (wlT_hi[:, :], bt_lo[:, cols])], True, True)
                last.then_inc(e_done, 1)

            def turn(t, i):
                running = tiled(t)
                if running:
                    y_half(t, i, 0, 0, 4)
                if tiled(t - 2):
                    pe.wait_ge(wlow_done, t - 1)
                    pe.transpose(o_ps[:, WLT:WLT + P], wlow[:, :], ident[:, :]).then_inc(wlt_done, 1)
                if running:
                    y_half(t, i, 0, 4, KC)
                if tiled(t - 2):
                    experts(t - 2)
                if running:
                    y_half(t, i, 1, 0, KC)
                if tiled(t - 1) and not (isinstance(t, int) and t > TILES):
                    x2_turn(t - 1, 0)
                    x2_turn(t - 1, 1)
                    low_rank(t - 1)

            turn(0, 0)
            turn(1, 1)
            turn(2, 0)
            turn(3, 1)
            with pe.Fori(4, TILES - 2, 2) as t:
                turn(t, 0)
                turn(t + 1, 1)
            for t in range(TILES - 2, TILES + 2):
                turn(t, t % 2)


def kernel(L0_attn_hidden_states, L0_attn_Wq, L0_attn_Wk, L0_attn_Wv, L0_attn_Wo, L0_ffn_A, L0_ffn_B, L0_ffn_Wr,
           L0_ffn_br):
    import numpy as np
    import concourse.bacc as bacc
    from concourse.bass_utils import run_bass_kernel_spmd

    def pair_blocks(w):
        w = np.asarray(w).reshape(KC, P, PAIRS, P)
        return w.transpose(2, 1, 0, 3).reshape(PAIRS, P, KC * P)

    wqkv = np.ascontiguousarray(np.stack([pair_blocks(w) for w in (L0_attn_Wq, L0_attn_Wk, L0_attn_Wv)]))
    a = np.asarray(L0_ffn_A).reshape(HR, EMBED)
    ar = np.concatenate([a, np.asarray(L0_ffn_Wr)], axis=0).T.reshape(KC, P, ARW).transpose(1, 0, 2)
    bt = np.asarray(L0_ffn_B).transpose(0, 2, 1).reshape(HR, EMBED)
    br = np.tile(np.asarray(L0_ffn_br)[None, :], (P, 1))

    inv = (np.float32(1.0) / np.float32(10000.0) ** (np.arange(0, DH, 2, dtype=np.float32) / np.float32(DH)))
    angle = np.tile(np.repeat(inv.astype(np.float32), 2), 2)[:, None] * np.arange(SEQ, dtype=np.float32)[None, :]
    arrays = {
        "x": np.ascontiguousarray(np.asarray(L0_attn_hidden_states).reshape(TOKENS, EMBED)),
        "wqkv": wqkv,
        "wo": np.ascontiguousarray(L0_attn_Wo),
        "ar": np.ascontiguousarray(ar),
        "bt": np.ascontiguousarray(bt),
        "br": np.ascontiguousarray(br),
        "cos": np.cos(angle).astype(np.float32),
        "sin": np.sin(angle).astype(np.float32),
    }
    nc = bacc.Bacc("TRN2", target_bir_lowering=False, num_devices=1)
    args = {n: nc.dram_tensor(f"in_{n}", a.shape, F32, kind="ExternalInput").ap() for n, a in arrays.items()}
    scratch = nc.dram_tensor("attention_out", (HEADS, DH, TOKENS), F32, kind="Internal").ap()
    out = nc.dram_tensor("out", (TOKENS, EMBED), F32, kind="ExternalOutput").ap()
    sandwich_kernel(nc, args["x"], args["wqkv"], args["wo"], args["ar"], args["bt"], args["br"], args["cos"],
                    args["sin"], scratch, out)
    r = run_bass_kernel_spmd(nc, [{f"in_{n}": a for n, a in arrays.items()}], core_ids=[0])
    return r.results[0]["out"].reshape(BATCHES, SEQ, EMBED)
```

```python
from contextlib import ExitStack

import concourse.bass as bass
from concourse import mybir

F32 = mybir.dt.float32
F32R = mybir.dt.float32r
ALU = mybir.AluOpType
ACT = mybir.ActivationFunctionType
AX = mybir.AxisListType

P = 128
EMBED = 1024
SEQ = 512
BATCHES = 4
HEADS = 16
DH = EMBED // HEADS
TOKENS = BATCHES * SEQ
KC = EMBED // P
PAIRS = HEADS // 2
QT = SEQ // P
STEPS = 2 * QT
HALVES = 2
UNITS = PAIRS * BATCHES
UPH = UNITS // HALVES
GROUP_MM = 3 * KC
MM_STEP = 3 * GROUP_MM // STEPS
TILES = TOKENS // P
EXPERTS = 8
RANK = 16
HR = EXPERTS * RANK
LOGITS = EXPERTS
WLT = 256
LN_STEPS = 5
ARW = HR + LOGITS
SCORE_SCALE = float(EXPERTS) * (32.0 / RANK)
EPS = 1e-5
MASKED = -1e30
SOFT = DH ** -0.5
CHUNKS = 8
SWAP = [p ^ 1 for p in range(32)]


def sandwich_kernel(nc, x, wqkv, wo, ar, bt, br, cos, sin, scratch, out):
    with ExitStack() as ctx:
        def sb(stack, name, shape, dt=F32):
            return stack.enter_context(nc.sbuf_tensor(name, shape, dt))

        def sem(name):
            return ctx.enter_context(nc.semaphore(name))

        bank = [ctx.enter_context(nc.psum_tensor(f"bank{i}", [P, 512], F32)) for i in range(8)]
        grp_ps = bank[0:2]
        sc_ps = bank[2:4]
        pt_ps = bank[4:6]
        o_ps = bank[6]
        tr_ps = bank[7]
        y_ps = [grp_ps, sc_ps]

        big_hi = sb(ctx, "big_hi", [P, 8192], F32R)
        big_lo = sb(ctx, "big_lo", [P, 8192], F32R)
        xT_hi = big_hi[:, :].rearrange("p (b c t) -> p b c t", b=2, c=KC)
        xT_lo = big_lo[:, :].rearrange("p (b c t) -> p b c t", b=2, c=KC)
        wo_hi = big_hi[:, :].rearrange("p (c n) -> p c n", c=KC)
        wo_lo = big_lo[:, :].rearrange("p (c n) -> p c n", c=KC)
        w_raw = sb(ctx, "w_raw", [P, 3, EMBED])
        w_hi = sb(ctx, "w_hi", [P, 3, EMBED], F32R)
        w_lo = sb(ctx, "w_lo", [P, 3, EMBED], F32R)
        oT_hi = w_hi[:, 0:2, :].rearrange("p i (c t) -> p i c t", c=KC)
        oT_lo = w_lo[:, 0:2, :].rearrange("p i (c t) -> p i c t", c=KC)
        xin = sb(ctx, "xin", [P, 2, EMBED])
        oT = xin[:, :, :].rearrange("p i (c t) -> p i c t", c=KC)
        ident = sb(ctx, "ident", [P, P])
        stats = sb(ctx, "stats", [P, 2, 6])
        mv = sb(ctx, "mv", [P, 2])
        ve = sb(ctx, "ve", [P, 1])
        lnv = sb(ctx, "lnv", [P, 1])
        r0 = sb(ctx, "r0", [P, 1])
        rr = sb(ctx, "rr", [P, 1])
        cc = sb(ctx, "cc", [P, 1])
        rstd = sb(ctx, "rstd", [P, 1])
        nmr = sb(ctx, "nmr", [P, 1])

        sB = ExitStack()
        qk_hi = sb(sB, "qk_hi", [P, 2, 2, SEQ], F32R)
        qk_lo = sb(sB, "qk_lo", [P, 2, 2, SEQ], F32R)
        v_hl = sb(sB, "v_hl", [P, 2, QT, 2, 2 * DH], F32R)
        mask = sb(sB, "mask", [P, SEQ])
        cos_sb = sb(sB, "cos_sb", [P, SEQ])
        sin_sb = sb(sB, "sin_sb", [P, SEQ])
        raw = sb(sB, "raw", [P, SEQ])
        swapped = sb(sB, "swapped", [P, SEQ])
        rot_c = sb(sB, "rot_c", [P, SEQ])
        rot_s = sb(sB, "rot_s", [P, SEQ])
        vraw = sb(sB, "vraw", [P, SEQ])
        neg = sb(sB, "neg", [P, 2, SEQ])
        prob = sb(sB, "prob", [P, 4, SEQ])
        pT_hi = sb(sB, "pT_hi", [P, 2, QT, SEQ], F32R)
        pT_lo = sb(sB, "pT_lo", [P, 2, QT, SEQ], F32R)
        nmax = sb(sB, "nmax", [P, 4])
        rsum = sb(sB, "rsum", [P, 4])
        rinv = sb(sB, "rinv", [P, 4])
        o_low = sb(sB, "o_low", [DH, SEQ])
        o_sum = sb(sB, "o_sum", [DH, 2, SEQ])
        xn = sb(sB, "xn", [P, 2, EMBED])
        wo_raw = [w_raw[:, 0, :], w_raw[:, 1, :], w_raw[:, 2, :], xn[:, 0, :], xn[:, 1, :]]
        sB.close()

        sC = ExitStack()
        ar_hi = sb(sC, "ar_hi", [P, KC, ARW], F32R)
        ar_lo = sb(sC, "ar_lo", [P, KC, ARW], F32R)
        bt_hi = sb(sC, "bt_hi", [P, EMBED], F32R)
        bt_lo = sb(sC, "bt_lo", [P, EMBED], F32R)
        ar_raw = sb(sC, "ar_raw", [P, KC, ARW])
        bt_raw = sb(sC, "bt_raw", [P, EMBED])
        br_sb = sb(sC, "br_sb", [P, LOGITS])
        xres = sb(sC, "xres", [P, 2, EMBED])
        x1 = sb(sC, "x1", [P, 2, EMBED])
        z = sb(sC, "z", [P, EMBED])
        xn2 = sb(sC, "xn2", [P, EMBED])
        x2T_hi = sb(sC, "x2T_hi", [P, KC, P], F32R)
        x2T_lo = sb(sC, "x2T_lo", [P, KC, P], F32R)
        logit = sb(sC, "logit", [P, LOGITS])
        lmax = sb(sC, "lmax", [P, 1])
        lexp = sb(sC, "lexp", [P, LOGITS])
        lsum = sb(sC, "lsum", [P, 1])
        linv = sb(sC, "linv", [P, 1])
        score = sb(sC, "score", [P, LOGITS])
        wlow = sb(sC, "wlow", [P, HR])
        wlT_hi = sb(sC, "wlT_hi", [P, P], F32R)
        wlT_lo = sb(sC, "wlT_lo", [P, P], F32R)
        res = sb(sC, "res", [P, 2, EMBED])
        sC.close()

        tables_in = sem("tables_in")
        x_in = [sem(f"x_in{i}") for i in range(2)]
        w_in = [sem(f"w_in{m}") for m in range(3)]
        consts = sem("consts")
        ln_stat = sem("ln_stat")
        ln_dve = sem("ln_dve")
        ln_act = sem("ln_act")
        normed = sem("normed")
        tr_done = sem("tr_done")
        tr_hi = sem("tr_hi")
        tr_lo = sem("tr_lo")
        w_hi_done = [sem(f"w_hi_done{m}") for m in range(3)]
        w_lo_done = [sem(f"w_lo_done{m}") for m in range(3)]
        grp_done = sem("grp_done")
        grp_read = sem("grp_read")
        swap_done = sem("swap_done")
        rot_mul = sem("rot_mul")
        rot_done = sem("rot_done")
        qk_hi_done = sem("qk_hi_done")
        qk_lo_done = sem("qk_lo_done")
        s_done = sem("s_done")
        neg_done = sem("neg_done")
        exp_done = sem("exp_done")
        inv_done = sem("inv_done")
        prob_done = sem("prob_done")
        t_done = sem("t_done")
        pt_hi_done = sem("pt_hi_done")
        pt_lo_done = sem("pt_lo_done")
        pv_done = sem("pv_done")
        olow_done = sem("olow_done")
        osum_done = sem("osum_done")
        o_out = [sem(f"o_out{i}") for i in range(2)]
        wo_in = [sem(f"wo_in{i}") for i in range(5)]
        wo_hi_done = sem("wo_hi_done")
        wo_lo_done = [sem(f"wo_lo_done{i}") for i in range(2)]
        ffn_in = sem("ffn_in")
        ffn_hi_done = sem("ffn_hi_done")
        ffn_lo_done = sem("ffn_lo_done")
        oT_in = [sem(f"oT_in{i}") for i in range(2)]
        xres_in = [sem(f"xres_in{i}") for i in range(2)]
        oT_hi_done = sem("oT_hi_done")
        oT_lo_done = sem("oT_lo_done")
        y_done = sem("y_done")
        x1_done = sem("x1_done")
        x2t_done = sem("x2t_done")
        x2T_hi_done = sem("x2T_hi_done")
        x2T_lo_done = sem("x2T_lo_done")
        low_done = sem("low_done")
        soft_dve = sem("soft_dve")
        soft_exp = sem("soft_exp")
        wlow_done = sem("wlow_done")
        wlt_done = sem("wlt_done")
        wlT_hi_done = sem("wlT_hi_done")
        wlT_lo_done = sem("wlT_lo_done")
        e_done = sem("e_done")
        res_done = sem("res_done")
        out_out = [sem(f"out_out{i}") for i in range(2)]

        gate_dve = sem("gate_dve")
        gate_pool = sem("gate_pool")

        block = ctx.enter_context(nc.Block())

        def late(count, first):
            return not isinstance(count, int) or count >= first

        def real(u):
            return not isinstance(u, int) or 0 <= u < UNITS

        def trailing(u, s, lag):
            at = s - lag
            a, q = u - 1 + at // STEPS, at % STEPS
            return a, q, STEPS * a + q

        def x_fill(batch, c):
            v_before = {0: 0, 1: 0, 2: UPH - 2, 3: UPH - 1}[batch] + (1 if batch >= 2 and c >= 2 else 0)
            return CHUNKS * batch + c + v_before

        def v_fill(u, half):
            chunks = 2 * CHUNKS if half == 0 else 4 * CHUNKS
            if isinstance(u, int):
                chunks = {UPH - 1: 2 * CHUNKS + 2, UPH: 3 * CHUNKS + 2}.get(u, 2 * CHUNKS if u < UPH else 4 * CHUNKS)
            return u - 1 + chunks

        def x_turns(u, s):
            if not isinstance(u, int):
                return 0, [], []
            now = {0: 1, UPH - 1: 2, UPH: 3}.get(u)
            nxt = {UPH - 2: 2, UPH - 1: 3}.get(u)
            tiles = []
            if now is not None and s in (1, 3):
                tiles.append(4 * now + (s + 3) // 2)
            if nxt is not None and s in (5, 7):
                tiles.append(4 * nxt + (s - 5) // 2)
            chunks = [[0], [1], [2, 3], [4], [5], [6], [7], []][s] if now is not None else []
            return now, tiles, chunks

        def run_slots(eng, slot):
            for half in range(HALVES):
                slot(0, 0, half)
                slot(0, 1, half)
                with eng.Fori(1, PAIRS - 1) as pair:
                    slot(pair, 0, half)
                    slot(pair, 1, half)
                slot(PAIRS - 1, 0, half)
                slot(PAIRS - 1, 1, half)
            slot(PAIRS, 0, 1)
            slot(PAIRS, 1, 1)

        def tiled(t):
            return not isinstance(t, int) or 0 <= t < TILES

        def ln_first(t):
            return TILES + 3 * t - 1 if late(t, 2) else TILES + 2 * t

        def ln_second(t):
            return ln_first(t) + 1

        def ln_third(t):
            return 4 * TILES - 1 if isinstance(t, int) and t == TILES - 1 else TILES + 3 * t + 4

        @block.sync
        def _(sp):
            def load_x(n):
                if n >= 2:
                    sp.wait_ge(normed, n - 1)
                sp.dma_start(xin[:, n % 2, :], x[n * P:(n + 1) * P, :]).then_inc(x_in[n % 2], 16)

            def load_w(m, n, pair):
                if late(n, 1):
                    sp.wait_ge(w_hi_done[m], n)
                    sp.wait_ge(w_lo_done[m], n)
                sp.dma_start(w_raw[:, m, :], wqkv[m, pair, :, :]).then_inc(w_in[m], 16)

            def store_o(u, pair, b, half, h):
                if real(u):
                    sp.wait_ge(osum_done, 2 * u + h + 1)
                    batch = 2 * half + b
                    sp.dma_start(scratch[2 * pair + h, :, batch * SEQ:(batch + 1) * SEQ],
                                 o_sum[:, h, :]).then_inc(o_out[h], 16)

            def load_wo(c):
                if c < 3:
                    sp.wait_ge(w_hi_done[c], 2 * PAIRS)
                    sp.wait_ge(w_lo_done[c], 2 * PAIRS)
                elif c == 3:
                    sp.wait_ge(tr_done, x_fill(3, CHUNKS - 1) + 1)
                elif c >= 5:
                    sp.wait_ge(wo_lo_done[(c - 5) % 2], (c - 5) // 2 + 1)
                sp.dma_start(wo_raw[c % 5], wo[c * P:(c + 1) * P, :]).then_inc(wo_in[c % 5], 16)

            def load_oT(t, i):
                if late(t, 2):
                    sp.wait_ge(oT_lo_done, t - 1)
                sp.dma_start(oT[:, i, :, :],
                             scratch.rearrange("(c h) d t -> (h d) c t", h=2)[:, :, bass.ds(t * P, P)]
                             ).then_inc(oT_in[i], 16)

            def load_xres(t, i):
                if late(t, 2):
                    sp.wait_ge(x1_done, t - 1)
                sp.dma_start(xres[:, i, :], x[bass.ds(t * P, P), :]).then_inc(xres_in[i], 16)

            load_x(0)
            load_w(0, 0, 0)
            load_x(1)
            sp.dma_start(cos_sb[:, :], cos).then_inc(tables_in, 16)
            sp.dma_start(sin_sb[:, :], sin).then_inc(tables_in, 16)
            load_w(1, 0, 0)
            load_w(2, 0, 0)
            for n in range(2, 6):
                load_x(n)

            def slot(pair, b, half):
                u = 2 * pair + b + UPH * half
                crossing = isinstance(pair, int) and pair == 0
                stored = (PAIRS - 1, half - 1) if crossing else (pair - 1, half)
                more = b == 0 and not (isinstance(u, int) and u >= UNITS - 2)
                n = pair + PAIRS * half + 1
                nxt = (pair + 1) % PAIRS if isinstance(pair, int) else pair + 1
                if more:
                    load_w(0, n, nxt)
                    load_w(1, n, nxt)
                store_o(u - 2, stored[0], b, stored[1], 0)
                early = {0: (6, 7), UPH - 2: (8, 9), UPH - 1: (10, 11), UPH: (14, 15)}
                for t in early.get(u, ()) if isinstance(u, int) else ():
                    load_x(t)
                if more:
                    load_w(2, n, nxt)
                if isinstance(u, int) and u == UNITS:
                    for c in range(5, KC):
                        load_wo(c)
                store_o(u - 2, stored[0], b, stored[1], 1)
                if isinstance(u, int) and u == UPH - 1:
                    load_x(12)
                    load_x(13)
                if isinstance(u, int) and u == UNITS - 1:
                    for c in range(5):
                        load_wo(c)
                    sp.wait_ge(normed, TILES)
                    for h in range(2):
                        sp.wait_ge(o_out[h], 16 * UPH)
                    load_oT(0, 0)
                    load_oT(1, 1)

            run_slots(sp, slot)

            sp.wait_ge(pv_done, HEADS * BATCHES)
            for h in range(2):
                sp.wait_ge(o_out[h], 16 * UNITS)
            load_xres(0, 0)
            sp.dma_start(ar_raw[:, :, :], ar).then_inc(ffn_in, 16)
            sp.dma_start(bt_raw[:, :], bt).then_inc(ffn_in, 16)
            sp.dma_start(br_sb[:, :], br).then_inc(ffn_in, 16)
            load_xres(1, 1)

            def turn(t, i):
                more = tiled(t + 2) and not (isinstance(t, int) and t >= TILES - 2)
                if more:
                    load_oT(t + 2, i)
                if tiled(t - 2):
                    sp.wait_ge(res_done, t - 1)
                    sp.dma_start(out[bass.ds((t - 2) * P, P), :], res[:, i, :]).then_inc(out_out[i], 16)
                if more:
                    load_xres(t + 2, i)

            turn(0, 0)
            turn(1, 1)
            with sp.Fori(2, TILES - 4, 2) as t:
                turn(t, 0)
                turn(t + 1, 1)
            for t in range(TILES - 4, TILES + 2):
                turn(t, t % 2)
            sp.wait_ge(out_out[0], 16 * TILES // 2)
            sp.wait_ge(out_out[1], 16 * TILES // 2)

        @block.gpsimd
        def _(pool):
            pool.memset(ident[:, :], 0.0).then_inc(consts, 1)
            pool.memset(mask[:, :], 0.0).then_inc(consts, 1)
            pool.wait_ge(consts, 2)
            pool.affine_select(out=ident[:, :], in_=ident[:, :], compare_op=ALU.not_equal, fill=1.0,
                               base=0, pattern=[[-1, P]], channel_multiplier=1).then_inc(consts, 1)
            diag = mask[:, SEQ - P:SEQ]
            pool.affine_select(out=diag, in_=diag, compare_op=ALU.is_ge, fill=MASKED,
                               base=0, pattern=[[-1, P]], channel_multiplier=1).then_inc(consts, 1)
            pool.wait_ge(tables_in, 32)

            def divide(u, s):
                a, q, g = trailing(u, s, 1)
                if real(a):
                    pool.wait_ge(inv_done, g + 1)
                    pool.sem_inc(gate_pool, 1)
                    p = prob[:, q % 4, 0:P * (q % QT + 1)]
                    pool.tensor_scalar(p, p, rinv[:, q % 4:q % 4 + 1], 1.0, ALU.mult, ALU.mult
                                       ).then_inc(prob_done, 1)

            def rotate(u, k):
                m = 2 * u + k
                pool.wait_ge(grp_read, 3 * u + k + 1)
                if late(m, 1):
                    pool.wait_ge(rot_done, m)
                    pool.wait_ge(qk_hi_done, m)
                    pool.wait_ge(qk_lo_done, m)
                pool.tensor_tensor(rot_c[:, :], raw[:, :], cos_sb[:, :], ALU.mult).then_inc(rot_mul, 1)
                pool.wait_ge(swap_done, m + 1)
                pool.tensor_tensor(rot_s[:, :], swapped[:, :], sin_sb[:, :], ALU.mult).then_inc(rot_mul, 1)

            def slot(pair, b, half):
                u = 2 * pair + b + UPH * half
                for s in range(STEPS):
                    divide(u, s)
                    if real(u) and s in (3, 6):
                        rotate(u, s // 6)
                    if isinstance(u, int) and u == UNITS and s % 2:
                        pool.wait_ge(wo_hi_done, s + 1)
                        pool.tensor_tensor(wo_lo[:, s, :], wo_raw[s % 5], wo_hi[:, s, :].bitcast(F32), ALU.subtract
                                           ).then_inc(wo_lo_done[1], 1)

            run_slots(pool, slot)

            def oT_low(t, i):
                pool.wait_ge(oT_hi_done, t + 1)
                pool.tensor_tensor(oT_lo[:, i, :, :], oT[:, i, :, :], oT_hi[:, i, :, :].bitcast(F32), ALU.subtract
                                   ).then_inc(oT_lo_done, 1)

            oT_low(0, 0)
            oT_low(1, 1)

            def turn(t, i):
                if tiled(t - 2):
                    pool.wait_ge(normed, ln_third(t - 2) + 1)
                    pool.tensor_tensor(res[:, i, :], res[:, i, :], x1[:, i, :], ALU.add).then_inc(res_done, 1)
                if tiled(t + 2) and not (isinstance(t, int) and t >= TILES - 2):
                    oT_low(t + 2, i)

            turn(0, 0)
            turn(1, 1)
            turn(2, 0)
            turn(3, 1)
            with pool.Fori(4, TILES - 2, 2) as t:
                turn(t, 0)
                turn(t + 1, 1)
            for t in range(TILES - 2, TILES + 2):
                turn(t, t % 2)

        @block.scalar
        def _(act):
            def ln_start(n):
                act.wait_ge(ln_dve, LN_STEPS * n + 1)
                act.activation(lnv[:, :], ve[:, :], ACT.Ln).then_inc(ln_act, 1)
                act.wait_ge(ln_act, 2 * n + 1)
                act.activation(r0[:, :], lnv[:, :], ACT.Exp, scale=-0.5).then_inc(ln_act, 1)

            def ln_rstd(n):
                ln_start(n)
                act.wait_ge(ln_dve, LN_STEPS * n + LN_STEPS)

            def normal(dst, src):
                return act.activation(dst, src, ACT.Identity, bias=nmr[:, 0:1], scale=rstd[:, 0:1])

            def x_tile(n):
                ln_rstd(n)
                if n >= 2:
                    act.wait_ge(tr_done, x_fill((n - 2) // 4, 2 * ((n - 2) % 4) + 1) + 1)
                normal(xn[:, n % 2, :], xin[:, n % 2, :]).then_inc(normed, 1)

            def x_chunk(batch, c):
                act.wait_ge(tr_done, x_fill(batch, c) + 1)
                if batch >= 2 and c == 0:
                    act.wait_ge(grp_done, 3 * (UPH - 3 + batch))
                dst = xT_hi[:, batch % 2, 4 * (c % 2):4 * (c % 2) + 4, P * (c // 2):P * (c // 2) + P]
                act.activation(dst, tr_ps[:, :].rearrange("p (c t) -> p c t", c=4), ACT.Copy).then_inc(tr_hi, 1)

            def w_high(m, n):
                act.wait_ge(w_in[m], 16 * n + 16)
                if late(n, 1):
                    act.wait_ge(grp_done, 6 * n - 2 + m)
                act.activation(w_hi[:, m, :], w_raw[:, m, :], ACT.Copy).then_inc(w_hi_done[m], 1)

            def exponent(u, s):
                a, q, g = trailing(u, s, 1)
                if real(a):
                    n = P * (q % QT + 1)
                    act.wait_ge(neg_done, g + 1)
                    if late(g, 4):
                        act.wait_ge(t_done, g - 3)
                    act.activation(prob[:, q % 4, 0:n], neg[:, q % 2, 0:n], ACT.Exp, scale=-1.0,
                                   bias=nmax[:, q % 4:q % 4 + 1], accum_out=rsum[:, q % 4:q % 4 + 1]
                                   ).then_inc(exp_done, 1)

            def pt_high(u, s):
                a, q, g = trailing(u, s, 3)
                if real(a):
                    i, h = q % QT, q // QT
                    act.wait_ge(t_done, g + 1)
                    if late(a, 1):
                        act.wait_ge(pv_done, 2 * a + h - 1)
                    act.activation(pT_hi[:, h, 0:i + 1, P * i:P * i + P],
                                   pt_ps[q % 2][:, 0:P * (i + 1)].rearrange("p (j t) -> p j t", j=i + 1),
                                   ACT.Copy).then_inc(pt_hi_done, 1)

            def qk_raw(u, b, k):
                m = 2 * u + k
                act.wait_ge(grp_done, 3 * u + k + 1)
                if late(m, 1):
                    act.wait_ge(rot_done, m)
                act.activation(raw[:, :], grp_ps[(b + k) % 2][:, :], ACT.Copy).then_inc(grp_read, 1)

            def qk_high(u, b, k):
                act.wait_ge(rot_done, 2 * u + k + 1)
                if late(u, 2):
                    act.wait_ge(s_done, STEPS * (u - 1))
                act.activation(qk_hi[:, b, k, :], rot_c[:, :], ACT.Copy).then_inc(qk_hi_done, 1)

            def v_raw(u, b, fill):
                act.wait_ge(grp_done, 3 * u + 3)
                act.wait_ge(tr_done, fill)
                act.activation(vraw[:, :], grp_ps[b][:, :], ACT.Copy).then_inc(grp_read, 1)

            def v_high(u, b, fill):
                act.wait_ge(tr_done, fill + 1)
                if late(u, 2):
                    act.wait_ge(pv_done, 2 * (u - 1))
                act.activation(v_hl[:, b, :, :, 0:DH].rearrange("p j h d -> p (j h) d"),
                               tr_ps[:, :].rearrange("p (j d) -> p j d", d=DH), ACT.Copy).then_inc(tr_hi, 1)

            def o_lower(a, h):
                n = 2 * a + h
                act.wait_ge(pv_done, n + 1)
                if late(n, 1):
                    act.wait_ge(osum_done, n)
                act.activation(o_low[:, :], o_ps[DH:2 * DH, :], ACT.Copy).then_inc(olow_done, 1)

            def slot(pair, b, half):
                u = 2 * pair + b + UPH * half
                n = pair + PAIRS * half
                fill = v_fill(u, half)
                for s in range(STEPS):
                    exponent(u, s)
                    if s == 0 and real(u - 1):
                        v_raw(u - 1, 1 - b, v_fill(u - 1, half) + 1)
                    if s == 1 and real(u - 2):
                        o_lower(u - 2, 0)
                    if s == 5 and real(u - 2):
                        o_lower(u - 2, 1)
                    if s == 2 and real(u - 1):
                        v_high(u - 1, 1 - b, fill)
                    pt_high(u, s)
                    if real(u):
                        if s == 2 and b == 0 and late(n, 1):
                            w_high(2, n)
                        if s == 3:
                            qk_raw(u, b, 0)
                        if s == 4:
                            qk_high(u, b, 0)
                        if s == 5:
                            qk_raw(u, b, 1)
                        if s == 7:
                            qk_high(u, b, 1)
                        if b == 1 and not (isinstance(u, int) and u == UNITS - 1):
                            if s == 4:
                                w_high(0, n + 1)
                            if s == 7:
                                w_high(1, n + 1)
                    batch, tiles, chunks = x_turns(u, s)
                    for c in chunks:
                        x_chunk(batch, c)
                    for t in tiles:
                        x_tile(t)
                    if isinstance(u, int) and u == UNITS:
                        wo_high(s)
                    if isinstance(u, int) and u == UNITS + 1 and s < 2:
                        oT_high(s, s, 16)

            def wo_high(c):
                act.wait_ge(grp_done, 3 * UNITS)
                act.wait_ge(wo_in[c % 5], 16 * (c // 5 + 1))
                act.activation(wo_hi[:, c, :], wo_raw[c % 5], ACT.Copy).then_inc(wo_hi_done, 1)

            def oT_high(t, i, count):
                act.wait_ge(oT_in[i], count)
                if late(t, 2):
                    act.wait_ge(y_done, t - 1)
                act.activation(oT_hi[:, i, :, :], oT[:, i, :, :], ACT.Copy).then_inc(oT_hi_done, 1)

            act.preload_act_table_set("natural_log_exp_and_others")
            x_tile(0)
            w_high(0, 0)
            for n in range(4):
                x_tile(n + 1)
                x_chunk(0, 2 * n)
                x_chunk(0, 2 * n + 1)
                if n < 2:
                    w_high(n + 1, 0)
            x_tile(5)
            run_slots(act, slot)

            act.wait_ge(pv_done, HEADS * BATCHES)
            act.wait_ge(osum_done, HEADS * BATCHES)

            def x2T_high(t, k):
                act.wait_ge(x2t_done, 2 * t + k + 1)
                if late(t, 1) and k == 0:
                    act.wait_ge(low_done, t)
                act.activation(x2T_hi[:, 4 * k:4 * k + 4, :], tr_ps[:, :].rearrange("p (c t) -> p c t", c=4),
                               ACT.Copy).then_inc(x2T_hi_done, 1)

            def turn(t, i):
                if tiled(t - 2):
                    ln_start(ln_third(t - 2))
                middle = tiled(t - 1) and not (isinstance(t, int) and t > TILES)
                if middle:
                    x2T_high(t - 1, 0)
                if tiled(t - 2):
                    act.wait_ge(ln_dve, LN_STEPS * (ln_third(t - 2) + 1))
                    if late(t, 4):
                        act.wait_ge(out_out[i], 8 * (t - i) - 16)
                    for k in range(2):
                        done = normal(res[:, i, 512 * k:512 * k + 512], pt_ps[k][:, :])
                    done.then_inc(normed, 1)
                if middle:
                    x2T_high(t - 1, 1)
                if tiled(t):
                    ln_start(ln_first(t))
                if middle:
                    act.wait_ge(soft_dve, 5 * (t - 1) + 2)
                    act.activation(lexp[:, :], logit[:, :], ACT.Exp, bias=lmax[:, 0:1],
                                   accum_out=lsum[:, 0:1]).then_inc(soft_exp, 1)
                if tiled(t):
                    act.wait_ge(ln_dve, LN_STEPS * (ln_first(t) + 1))
                    for k in range(2):
                        done = normal(z[:, 512 * k:512 * k + 512], y_ps[i][k][:, :])
                    done.then_inc(normed, 1)
                if tiled(t + 2) and not (isinstance(t, int) and t >= TILES - 2):
                    oT_high(t + 2, i, 8 * (t + 2 - i) + 16)
                if middle:
                    act.wait_ge(wlt_done, t)
                    if late(t, 2):
                        act.wait_ge(e_done, t - 1)
                    act.activation(wlT_hi[:, :], o_ps[:, WLT:WLT + P], ACT.Copy).then_inc(wlT_hi_done, 1)
                if tiled(t):
                    ln_rstd(ln_second(t))
                    normal(xn2[:, :], x1[:, i, :]).then_inc(normed, 1)
                if isinstance(t, int) and t == 0:
                    act.wait_ge(ffn_in, 48)
                    act.activation(ar_hi[:, :, :], ar_raw[:, :, :], ACT.Copy).then_inc(ffn_hi_done, 1)
                    act.activation(bt_hi[:, :], bt_raw[:, :], ACT.Copy).then_inc(ffn_hi_done, 1)

            turn(0, 0)
            turn(1, 1)
            turn(2, 0)
            turn(3, 1)
            with act.Fori(4, TILES - 2, 2) as t:
                turn(t, 0)
                turn(t + 1, 1)
            for t in range(TILES - 2, TILES + 2):
                turn(t, t % 2)

        @block.vector
        def _(dve):
            def ln_stats(src):
                dve.bn_stats(stats[:, 0, :], src[0]).then_inc(ln_stat, 1)
                dve.bn_stats(stats[:, 1, :], src[1]).then_inc(ln_stat, 1)

            def layernorm(n, src):
                ln_stats(src)
                ln_variance(n)
                ln_scale(n)

            def ln_variance(n):
                dve.wait_ge(ln_stat, 3 * n + 2)
                dve.sem_inc(gate_dve, 1)
                dve.bn_aggr(mv[:, :], stats[:, :, :].rearrange("p a b -> p (a b)")).then_inc(ln_stat, 1)
                dve.wait_ge(ln_stat, 3 * n + 3)
                dve.tensor_scalar(ve[:, :], mv[:, 1:2], EPS, None, ALU.add).then_inc(ln_dve, 1)

            def ln_scale(n):
                dve.wait_ge(ln_act, 2 * n + 2)
                dve.wait_ge(ln_dve, LN_STEPS * n + 1)
                dve.scalar_tensor_tensor(out=rr[:, :], in0=r0[:, :], scalar=ve[:, 0:1], in1=r0[:, :],
                                         op0=ALU.mult, op1=ALU.mult).then_inc(ln_dve, 1)
                dve.wait_ge(ln_dve, LN_STEPS * n + 2)
                dve.tensor_scalar(cc[:, :], rr[:, :], -0.5, 1.5, ALU.mult, ALU.add).then_inc(ln_dve, 1)
                if late(n, 1):
                    dve.wait_ge(normed, n)
                dve.wait_ge(ln_dve, LN_STEPS * n + 3)
                dve.tensor_tensor(rstd[:, :], cc[:, :], r0[:, :], ALU.mult).then_inc(ln_dve, 1)
                dve.wait_ge(ln_dve, LN_STEPS * n + 4)
                dve.scalar_tensor_tensor(out=nmr[:, :], in0=mv[:, 0:1], scalar=-1.0, in1=rstd[:, :],
                                         op0=ALU.mult, op1=ALU.mult).then_inc(ln_dve, 1)

            def x_tile(n):
                dve.wait_ge(x_in[n % 2], 16 * (n // 2 + 1))
                layernorm(n, [xin[:, n % 2, 0:512], xin[:, n % 2, 512:1024]])

            def x_chunk(batch, c):
                dve.wait_ge(tr_hi, x_fill(batch, c) + 1)
                at = (slice(None), batch % 2, slice(4 * (c % 2), 4 * (c % 2) + 4),
                      slice(P * (c // 2), P * (c // 2) + P))
                dve.tensor_tensor(xT_lo[at], tr_ps[:, :].rearrange("p (c t) -> p c t", c=4),
                                  xT_hi[at].bitcast(F32), ALU.subtract).then_inc(tr_lo, 1)

            def w_low(m, n):
                dve.wait_ge(w_hi_done[m], n + 1)
                dve.tensor_tensor(w_lo[:, m, :], w_raw[:, m, :], w_hi[:, m, :].bitcast(F32), ALU.subtract
                                  ).then_inc(w_lo_done[m], 1)

            def negate(u, s):
                a, q, g = trailing(u, s, 1)
                if real(a):
                    n = P * (q % QT + 1)
                    dve.wait_ge(s_done, g + 1)
                    if late(g, 2):
                        dve.wait_ge(exp_done, g - 1)
                    dve.sem_inc(gate_dve, 1)
                    dve.tensor_tensor_reduce(neg[:, q % 2, 0:n], sc_ps[q % 2][:, 0:n], mask[:, SEQ - n:SEQ],
                                             -SOFT, 3e38, ALU.add, ALU.min, nmax[:, q % 4:q % 4 + 1]
                                             ).then_inc(neg_done, 1)

            def invert(u, s):
                a, q, g = trailing(u, s, 1)
                if real(a):
                    dve.wait_ge(exp_done, g + 1)
                    if late(g, 4):
                        dve.wait_ge(prob_done, g - 3)
                    dve.reciprocal(rinv[:, q % 4:q % 4 + 1], rsum[:, q % 4:q % 4 + 1]).then_inc(inv_done, 1)

            def pt_low(u, s):
                a, q, g = trailing(u, s, 3)
                if real(a):
                    i, h = q % QT, q // QT
                    dve.wait_ge(pt_hi_done, g + 1)
                    at = (slice(None), h, slice(0, i + 1), slice(P * i, P * i + P))
                    dve.tensor_tensor(pT_lo[at], pt_ps[q % 2][:, 0:P * (i + 1)].rearrange("p (j t) -> p j t", j=i + 1),
                                      pT_hi[at].bitcast(F32), ALU.subtract).then_inc(pt_lo_done, 1)

            def swap(u, k):
                m = 2 * u + k
                dve.wait_ge(grp_read, 3 * u + k + 1)
                if late(m, 1):
                    dve.wait_ge(rot_mul, 2 * m)
                dve.sem_inc(gate_dve, 1)
                dve.stream_shuffle(swapped[:, :], raw[:, :], SWAP).then_inc(swap_done, 1)

            def rotate(u, k):
                m = 2 * u + k
                dve.wait_ge(rot_mul, 2 * m + 2)
                dve.tensor_tensor(rot_c[:, :], rot_c[:, :], rot_s[:, :], ALU.add).then_inc(rot_done, 1)

            def qk_low(u, b, k):
                dve.wait_ge(qk_hi_done, 2 * u + k + 1)
                dve.tensor_tensor(qk_lo[:, b, k, :], rot_c[:, :], qk_hi[:, b, k, :].bitcast(F32), ALU.subtract
                                  ).then_inc(qk_lo_done, 1)

            def v_low(b, fill):
                dve.wait_ge(tr_hi, fill + 1)
                dve.tensor_tensor(v_hl[:, b, :, :, DH:2 * DH].rearrange("p j h d -> p (j h) d"),
                                  tr_ps[:, :].rearrange("p (j d) -> p j d", d=DH),
                                  v_hl[:, b, :, :, 0:DH].rearrange("p j h d -> p (j h) d").bitcast(F32),
                                  ALU.subtract).then_inc(tr_lo, 1)

            def o_add(a, h):
                dve.wait_ge(olow_done, 2 * a + h + 1)
                if late(a, 1):
                    dve.wait_ge(o_out[h], 16 * a)
                dve.tensor_tensor(o_sum[:, h, :], o_ps[0:DH, :], o_low[:, :], ALU.add).then_inc(osum_done, 1)

            def slot(pair, b, half):
                u = 2 * pair + b + UPH * half
                n = pair + PAIRS * half
                fill = v_fill(u, half)
                for s in range(STEPS):
                    negate(u, s)
                    if s == 0 and real(u - 1):
                        qk_low(u - 1, 1 - b, 1)
                    if s == 1 and real(u - 2):
                        o_add(u - 2, 0)
                    if s == 5 and real(u - 2):
                        o_add(u - 2, 1)
                    if real(u):
                        if s == 3:
                            swap(u, 0)
                        if s == 4:
                            rotate(u, 0)
                        if s == 6:
                            swap(u, 1)
                        if s == 7:
                            rotate(u, 1)
                    invert(u, s)
                    if s == 2 and real(u - 1):
                        v_low(1 - b, fill)
                    pt_low(u, s)
                    if real(u):
                        if s == 3 and b == 0 and late(n, 1):
                            w_low(2, n)
                        if s == 4:
                            qk_low(u, b, 0)
                        if b == 1 and not (isinstance(u, int) and u == UNITS - 1):
                            if s == 5:
                                w_low(0, n + 1)
                            if s == 7:
                                w_low(1, n + 1)
                    batch, tiles, chunks = x_turns(u, s)
                    for c in chunks:
                        x_chunk(batch, c)
                    for t in tiles:
                        x_tile(t)
                    if isinstance(u, int) and u == UNITS and s % 2 == 0:
                        dve.wait_ge(wo_hi_done, s + 1)
                        dve.tensor_tensor(wo_lo[:, s, :], wo_raw[s % 5], wo_hi[:, s, :].bitcast(F32), ALU.subtract
                                          ).then_inc(wo_lo_done[0], 1)

            dve.wait_ge(consts, 4)
            x_tile(0)
            w_low(0, 0)
            for n in range(4):
                x_tile(n + 1)
                x_chunk(0, 2 * n)
                x_chunk(0, 2 * n + 1)
                if n < 2:
                    w_low(n + 1, 0)
            x_tile(5)
            run_slots(dve, slot)

            dve.wait_ge(pv_done, HEADS * BATCHES)
            for h in range(2):
                dve.wait_ge(o_out[h], 16 * UNITS)

            def turn(t, i):
                middle = tiled(t - 1) and not (isinstance(t, int) and t > TILES)
                if tiled(t - 2):
                    dve.wait_ge(e_done, t - 1)
                    layernorm(ln_third(t - 2), [e[:, :] for e in pt_ps])
                if middle:
                    for k in range(2):
                        dve.wait_ge(x2T_hi_done, 2 * (t - 1) + k + 1)
                        dve.tensor_tensor(x2T_lo[:, 4 * k:4 * k + 4, :],
                                          tr_ps[:, :].rearrange("p (c t) -> p c t", c=4),
                                          x2T_hi[:, 4 * k:4 * k + 4, :].bitcast(F32), ALU.subtract
                                          ).then_inc(x2T_lo_done, 1)
                if tiled(t):
                    dve.wait_ge(y_done, t + 1)
                    ln_stats([y[:, :] for y in y_ps[i]])
                    ln_variance(ln_first(t))
                if middle:
                    m = 5 * (t - 1)
                    dve.wait_ge(low_done, t)
                    dve.tensor_tensor(logit[:, :], o_ps[:, HR:ARW], br_sb[:, :], ALU.add).then_inc(soft_dve, 1)
                    dve.wait_ge(soft_dve, m + 1)
                    dve.tensor_reduce(lmax[:, :], logit[:, :], AX.X, ALU.max, negate=True).then_inc(soft_dve, 1)
                if tiled(t):
                    ln_scale(ln_first(t))
                if middle:
                    dve.wait_ge(soft_exp, t)
                    dve.reciprocal(linv[:, :], lsum[:, :]).then_inc(soft_dve, 1)
                    dve.wait_ge(soft_dve, m + 3)
                    dve.tensor_scalar(score[:, :], lexp[:, :], linv[:, 0:1], SCORE_SCALE, ALU.mult, ALU.mult
                                      ).then_inc(soft_dve, 2)
                    dve.wait_ge(soft_dve, m + 5)
                    if late(t, 2):
                        dve.wait_ge(wlt_done, t - 1)
                    dve.tensor_tensor(wlow[:, :].rearrange("p (h r) -> p h r", h=EXPERTS),
                                      o_ps[:, 0:HR].rearrange("p (h r) -> p h r", h=EXPERTS),
                                      score[:, :].rearrange("p (h o) -> p h o", o=1).to_broadcast([P, EXPERTS, RANK]),
                                      ALU.mult).then_inc(wlow_done, 1)
                if tiled(t):
                    dve.wait_ge(normed, ln_first(t) + 1)
                    dve.wait_ge(xres_in[i], 8 * (t - i) + 16)
                    if late(t, 2):
                        dve.wait_ge(res_done, t - 1)
                    dve.tensor_tensor(x1[:, i, :], z[:, :], xres[:, i, :], ALU.add).then_inc(x1_done, 1)
                if middle:
                    dve.wait_ge(wlT_hi_done, t)
                    dve.tensor_tensor(wlT_lo[:, :], o_ps[:, WLT:WLT + P], wlT_hi[:, :].bitcast(F32), ALU.subtract
                                      ).then_inc(wlT_lo_done, 1)
                if tiled(t):
                    dve.wait_ge(x1_done, t + 1)
                    layernorm(ln_second(t), [x1[:, i, 0:512], x1[:, i, 512:1024]])
                if isinstance(t, int) and t == 0:
                    dve.wait_ge(ffn_hi_done, 2)
                    dve.tensor_tensor(ar_lo[:, :, :], ar_raw[:, :, :], ar_hi[:, :, :].bitcast(F32), ALU.subtract
                                      ).then_inc(ffn_lo_done, 1)
                    dve.tensor_tensor(bt_lo[:, :], bt_raw[:, :], bt_hi[:, :].bitcast(F32), ALU.subtract
                                      ).then_inc(ffn_lo_done, 1)

            turn(0, 0)
            turn(1, 1)
            turn(2, 0)
            turn(3, 1)
            with dve.Fori(4, TILES - 2, 2) as t:
                turn(t, 0)
                turn(t + 1, 1)
            for t in range(TILES - 2, TILES + 2):
                turn(t, t % 2)

        @block.tensor
        def _(pe):
            def products(dst, terms, first, last):
                for n, (lhsT, rhs) in enumerate(terms):
                    mm = pe.matmul(dst, lhsT, rhs, start=first and n == 0, stop=last and n == len(terms) - 1)
                return mm

            def x_chunk(batch, c):
                f = x_fill(batch, c)
                pe.wait_ge(normed, 4 * batch + c // 2 + 1)
                if f:
                    pe.wait_ge(tr_hi, f)
                    pe.wait_ge(tr_lo, f)
                for k in range(4):
                    col = P * (4 * (c % 2) + k)
                    last = pe.transpose(tr_ps[:, P * k:P * k + P], xn[:, c // 2 % 2, col:col + P], ident[:, :])
                last.then_inc(tr_done, 1)

            def v_turn(u, fill):
                pe.wait_ge(grp_read, 3 * u + 3)
                pe.wait_ge(tr_hi, fill)
                pe.wait_ge(tr_lo, fill)
                for k in range(QT):
                    last = pe.transpose(tr_ps[:, P * k:P * k + P], vraw[:, P * k:P * k + P], ident[:, :])
                last.then_inc(tr_done, 1)

            def project(u, b, n, half, first, count):
                for mm in range(first, first + count):
                    k, at = mm // GROUP_MM, mm % GROUP_MM
                    c, part = at // 3, at % 3
                    if at == 0:
                        pe.wait_ge(w_hi_done[k], n + 1)
                        pe.wait_ge(w_lo_done[k], n + 1)
                        if late(3 * u + k, 2):
                            pe.wait_ge(grp_read, 3 * u + k - 1)
                        if isinstance(u, int) and u in (0, 1, UPH, UPH + 1) and k == 0:
                            f = x_fill(2 * half + b, CHUNKS - 1) + 1
                            pe.wait_ge(tr_hi, f)
                            pe.wait_ge(tr_lo, f)
                    w = (w_lo if part == 2 else w_hi)[:, k, P * c:P * c + P]
                    xt = (xT_lo if part == 1 else xT_hi)[:, b, c, :]
                    done = pe.matmul(grp_ps[(b + k) % 2][:, :], w, xt, start=at == 0, stop=at == GROUP_MM - 1)
                    if at == GROUP_MM - 1:
                        done.then_inc(grp_done, 1)

            def scores(u, s, b):
                a, q, g = trailing(u, s, 1)
                if real(a):
                    ab = (b + 1 + (s - 1) // STEPS) % 2
                    i, h = q % QT, q // QT
                    if q == 0:
                        pe.wait_ge(qk_lo_done, 2 * a + 2)
                        pe.wait_ge(qk_hi_done, 2 * a + 2)
                    if late(g, 2):
                        pe.wait_ge(neg_done, g - 1)
                    rows = slice(DH * h, DH * h + DH)
                    qc, kc = slice(P * i, P * i + P), slice(0, P * i + P)
                    q_hi, q_lo = qk_hi[rows, ab, 0, qc], qk_lo[rows, ab, 0, qc]
                    k_hi, k_lo = qk_hi[rows, ab, 1, kc], qk_lo[rows, ab, 1, kc]
                    products(sc_ps[q % 2][:, kc], [(q_hi, k_hi), (q_hi, k_lo), (q_lo, k_hi)], True, True
                             ).then_inc(s_done, 1)

            def turn_probs(u, s):
                a, q, g = trailing(u, s, 3)
                if real(a):
                    pe.wait_ge(prob_done, g + 1)
                    if late(g, 2):
                        pe.wait_ge(pt_hi_done, g - 1)
                        pe.wait_ge(pt_lo_done, g - 1)
                    for j in range(q % QT + 1):
                        last = pe.transpose(pt_ps[q % 2][:, P * j:P * j + P], prob[:, q % 4, P * j:P * j + P],
                                            ident[:, :])
                    last.then_inc(t_done, 1)

            def attend(a, b, h, fill):
                if real(a):
                    g = STEPS * a + QT * h + QT - 1
                    pe.wait_ge(pt_hi_done, g + 1)
                    pe.wait_ge(pt_lo_done, g + 1)
                    if h == 0:
                        pe.wait_ge(tr_hi, fill)
                        pe.wait_ge(tr_lo, fill)
                    if late(2 * a + h, 1):
                        pe.wait_ge(osum_done, 2 * a + h)
                    for j in range(QT):
                        cols = slice(P * j, SEQ)
                        v = v_hl[:, b, j, h, :]
                        last = products(o_ps[:, cols], [(v, pT_hi[:, h, j, cols]), (v, pT_lo[:, h, j, cols])],
                                        j == 0, j == QT - 1)
                    last.then_inc(pv_done, 1)

            def y_half(t, i, k, c0, c1):
                if k == 0 and c0 == 0:
                    if isinstance(t, int) and t == 0:
                        pe.wait_ge(grp_read, 3 * UNITS)
                    pe.wait_ge(oT_hi_done, t + 1)
                    pe.wait_ge(oT_lo_done, t + 1)
                    if late(t, 2):
                        pe.wait_ge(normed, ln_first(t - 2) + 1)
                for c in range(c0, c1):
                    if isinstance(t, int) and t == 0 and k == 0:
                        pe.wait_ge(wo_hi_done, c + 1)
                        pe.wait_ge(wo_lo_done[c % 2], c // 2 + 1)
                    cols = slice(512 * k, 512 * k + 512)
                    last = products(y_ps[i][k][:, :], [(oT_hi[:, i, c, :], wo_hi[:, c, cols]),
                                                       (oT_lo[:, i, c, :], wo_hi[:, c, cols]),
                                                       (oT_hi[:, i, c, :], wo_lo[:, c, cols])], c == 0, c == KC - 1)
                if k == 1 and c1 == KC:
                    last.then_inc(y_done, 1)

            def slot(pair, b, half):
                u = 2 * pair + b + UPH * half
                n = pair + PAIRS * half
                fill = v_fill(u, half)
                for s in range(STEPS):
                    third = MM_STEP // 3

                    def project_third(k):
                        if real(u):
                            project(u, b, n, half, MM_STEP * s + third * k, third)

                    project_third(0)
                    if s == 2 and real(u - 1):
                        v_turn(u - 1, fill)
                    scores(u, s, b)
                    project_third(1)
                    turn_probs(u, s)
                    project_third(2)
                    if s == 0:
                        attend(u - 2, b, 0, v_fill(u - 1, half) + 1)
                    if s == 4:
                        attend(u - 2, b, 1, None)
                    batch, _, chunks = x_turns(u, s)
                    for c in chunks:
                        x_chunk(batch, c)
                    if isinstance(u, int) and u == UNITS + 1 and s < 4:
                        y_half(0, 0, s // 2, 4 * (s % 2), 4 * (s % 2) + 4)

            pe.wait_ge(consts, 4)
            for c in range(CHUNKS):
                x_chunk(0, c)
            run_slots(pe, slot)

            pe.wait_ge(neg_done, STEPS * UNITS)
            pe.wait_ge(osum_done, HEADS * BATCHES)

            def x2_turn(t, k):
                if k == 0:
                    pe.wait_ge(normed, ln_second(t) + 1)
                if late(2 * t + k, 1):
                    pe.wait_ge(x2T_hi_done, 2 * t + k)
                    pe.wait_ge(x2T_lo_done, 2 * t + k)
                for c in range(4):
                    last = pe.transpose(tr_ps[:, P * c:P * c + P], xn2[:, P * (4 * k + c):P * (4 * k + c) + P],
                                        ident[:, :])
                last.then_inc(x2t_done, 1)

            def low_rank(t):
                if isinstance(t, int) and t == 0:
                    pe.wait_ge(ffn_lo_done, 2)
                if late(t, 1):
                    pe.wait_ge(wlT_hi_done, t)
                    pe.wait_ge(wlT_lo_done, t)
                for c in range(KC):
                    if c % 4 == 0:
                        pe.wait_ge(x2T_hi_done, 2 * t + c // 4 + 1)
                        pe.wait_ge(x2T_lo_done, 2 * t + c // 4 + 1)
                    last = products(o_ps[:, 0:ARW], [(x2T_hi[:, c, :], ar_hi[:, c, :]), (x2T_lo[:, c, :], ar_hi[:, c, :]),
                                                     (x2T_hi[:, c, :], ar_lo[:, c, :])], c == 0, c == KC - 1)
                last.then_inc(low_done, 1)

            def experts(t):
                pe.wait_ge(wlT_hi_done, t + 1)
                pe.wait_ge(wlT_lo_done, t + 1)
                if late(t, 1):
                    pe.wait_ge(normed, ln_third(t - 1) + 1)
                for k in range(2):
                    cols = slice(512 * k, 512 * k + 512)
                    last = products(pt_ps[k][:, :], [(wlT_hi[:, :], bt_hi[:, cols]), (wlT_lo[:, :], bt_hi[:, cols]),
                                                     (wlT_hi[:, :], bt_lo[:, cols])], True, True)
                last.then_inc(e_done, 1)

            def turn(t, i):
                running = tiled(t) and not (isinstance(t, int) and t == 0)
                middle = tiled(t - 1) and not (isinstance(t, int) and t > TILES)
                if running:
                    y_half(t, i, 0, 0, 5)
                if tiled(t - 2):
                    pe.wait_ge(wlow_done, t - 1)
                    pe.transpose(o_ps[:, WLT:WLT + P], wlow[:, :], ident[:, :]).then_inc(wlt_done, 1)
                if running:
                    y_half(t, i, 0, 5, KC)
                if tiled(t - 2):
                    experts(t - 2)
                if running:
                    y_half(t, i, 1, 0, 4)
                if middle:
                    x2_turn(t - 1, 0)
                if running:
                    y_half(t, i, 1, 4, 7)
                if middle:
                    x2_turn(t - 1, 1)
                if running:
                    y_half(t, i, 1, 7, KC)
                if middle:
                    low_rank(t - 1)

            turn(0, 0)
            turn(1, 1)
            turn(2, 0)
            turn(3, 1)
            with pe.Fori(4, TILES - 2, 2) as t:
                turn(t, 0)
                turn(t + 1, 1)
            for t in range(TILES - 2, TILES + 2):
                turn(t, t % 2)


def kernel(L0_attn_hidden_states, L0_attn_Wq, L0_attn_Wk, L0_attn_Wv, L0_attn_Wo, L0_ffn_A, L0_ffn_B, L0_ffn_Wr,
           L0_ffn_br):
    import numpy as np
    import concourse.bacc as bacc
    from concourse.bass_utils import run_bass_kernel_spmd

    def pair_blocks(w):
        w = np.asarray(w).reshape(KC, P, PAIRS, P)
        return w.transpose(2, 1, 0, 3).reshape(PAIRS, P, KC * P)

    wqkv = np.ascontiguousarray(np.stack([pair_blocks(w) for w in (L0_attn_Wq, L0_attn_Wk, L0_attn_Wv)]))
    a = np.asarray(L0_ffn_A).reshape(HR, EMBED)
    ar = np.concatenate([a, np.asarray(L0_ffn_Wr)], axis=0).T.reshape(KC, P, ARW).transpose(1, 0, 2)
    bt = np.asarray(L0_ffn_B).transpose(0, 2, 1).reshape(HR, EMBED)
    br = np.tile(np.asarray(L0_ffn_br)[None, :], (P, 1))

    inv = (np.float32(1.0) / np.float32(10000.0) ** (np.arange(0, DH, 2, dtype=np.float32) / np.float32(DH)))
    angle = np.tile(np.repeat(inv.astype(np.float32), 2), 2)[:, None] * np.arange(SEQ, dtype=np.float32)[None, :]
    arrays = {
        "x": np.ascontiguousarray(np.asarray(L0_attn_hidden_states).reshape(TOKENS, EMBED)),
        "wqkv": wqkv,
        "wo": np.ascontiguousarray(L0_attn_Wo),
        "ar": np.ascontiguousarray(ar),
        "bt": np.ascontiguousarray(bt),
        "br": np.ascontiguousarray(br),
        "cos": np.cos(angle).astype(np.float32),
        "sin": np.sin(angle).astype(np.float32),
    }
    nc = bacc.Bacc("TRN2", target_bir_lowering=False, num_devices=1)
    args = {n: nc.dram_tensor(f"in_{n}", a.shape, F32, kind="ExternalInput").ap() for n, a in arrays.items()}
    scratch = nc.dram_tensor("attention_out", (HEADS, DH, TOKENS), F32, kind="Internal").ap()
    out = nc.dram_tensor("out", (TOKENS, EMBED), F32, kind="ExternalOutput").ap()
    sandwich_kernel(nc, args["x"], args["wqkv"], args["wo"], args["ar"], args["bt"], args["br"], args["cos"],
                    args["sin"], scratch, out)
    r = run_bass_kernel_spmd(nc, [{f"in_{n}": a for n, a in arrays.items()}], core_ids=[0])
    return r.results[0]["out"].reshape(BATCHES, SEQ, EMBED)
```

```python
from contextlib import ExitStack

import concourse.bass as bass
from concourse import mybir

F32 = mybir.dt.float32
F32R = mybir.dt.float32r
ALU = mybir.AluOpType
ACT = mybir.ActivationFunctionType
AX = mybir.AxisListType

P = 128
EMBED = 1024
SEQ = 512
BATCHES = 4
HEADS = 16
DH = EMBED // HEADS
TOKENS = BATCHES * SEQ
KC = EMBED // P
PAIRS = HEADS // 2
QT = SEQ // P
STEPS = 2 * QT
HALVES = 2
UNITS = PAIRS * BATCHES
UPH = UNITS // HALVES
GROUP_MM = 3 * KC
MM_STEP = 3 * GROUP_MM // STEPS
TILES = TOKENS // P
EXPERTS = 8
RANK = 16
HR = EXPERTS * RANK
LOGITS = EXPERTS
WLT = 256
LN_STEPS = 5
ARW = HR + LOGITS
SCORE_SCALE = float(EXPERTS) * (32.0 / RANK)
EPS = 1e-5
MASKED = -1e30
SOFT = DH ** -0.5
CHUNKS = 8
SWAP = [p ^ 1 for p in range(32)]


def sandwich_kernel(nc, x, wqkv, wo, ar, bt, br, cos, sin, scratch, out):
    with ExitStack() as ctx:
        def sb(stack, name, shape, dt=F32):
            return stack.enter_context(nc.sbuf_tensor(name, shape, dt))

        def sem(name):
            return ctx.enter_context(nc.semaphore(name))

        bank = [ctx.enter_context(nc.psum_tensor(f"bank{i}", [P, 512], F32)) for i in range(8)]
        grp_ps = bank[0:2]
        sc_ps = bank[2:4]
        pt_ps = bank[4:6]
        o_ps = bank[6]
        tr_ps = bank[7]
        y_ps = [grp_ps, sc_ps]

        big_hi = sb(ctx, "big_hi", [P, 8192], F32R)
        big_lo = sb(ctx, "big_lo", [P, 8192], F32R)
        xT_hi = big_hi[:, :].rearrange("p (b c t) -> p b c t", b=2, c=KC)
        xT_lo = big_lo[:, :].rearrange("p (b c t) -> p b c t", b=2, c=KC)
        wo_hi = big_hi[:, :].rearrange("p (c n) -> p c n", c=KC)
        wo_lo = big_lo[:, :].rearrange("p (c n) -> p c n", c=KC)
        w_raw = sb(ctx, "w_raw", [P, 3, EMBED])
        w_hi = sb(ctx, "w_hi", [P, 3, EMBED], F32R)
        w_lo = sb(ctx, "w_lo", [P, 3, EMBED], F32R)
        oT_hi = w_hi[:, 0:2, :].rearrange("p i (c t) -> p i c t", c=KC)
        oT_lo = w_lo[:, 0:2, :].rearrange("p i (c t) -> p i c t", c=KC)
        xin = sb(ctx, "xin", [P, 2, EMBED])
        oT = xin[:, :, :].rearrange("p i (c t) -> p i c t", c=KC)
        ident = sb(ctx, "ident", [P, P])
        stats = sb(ctx, "stats", [P, 2, 6])
        mv = sb(ctx, "mv", [P, 2])
        ve = sb(ctx, "ve", [P, 1])
        lnv = sb(ctx, "lnv", [P, 1])
        r0 = sb(ctx, "r0", [P, 1])
        rr = sb(ctx, "rr", [P, 1])
        cc = sb(ctx, "cc", [P, 1])
        rstd = sb(ctx, "rstd", [P, 1])
        nmr = sb(ctx, "nmr", [P, 1])

        sB = ExitStack()
        q_hl = sb(sB, "q_hl", [P, 2, 2, SEQ], F32R)
        k_hh = sb(sB, "k_hh", [P, 2, 2, SEQ], F32R)
        k_lo = sb(sB, "k_lo", [P, 2, SEQ], F32R)
        v_hl = sb(sB, "v_hl", [P, 2, QT, 2, 2 * DH], F32R)
        mask = sb(sB, "mask", [P, SEQ])
        cos_sb = sb(sB, "cos_sb", [P, SEQ])
        sin_sb = sb(sB, "sin_sb", [P, SEQ])
        raw = sb(sB, "raw", [P, SEQ])
        swapped = sb(sB, "swapped", [P, SEQ])
        rot_c = sb(sB, "rot_c", [P, SEQ])
        neg = sb(sB, "neg", [P, 2, SEQ])
        prob = sb(sB, "prob", [P, 4, SEQ])
        pT_hi = sb(sB, "pT_hi", [P, 2, QT, SEQ], F32R)
        pT_lo = sb(sB, "pT_lo", [P, 2, QT, SEQ], F32R)
        nmax = sb(sB, "nmax", [P, 4])
        rsum = sb(sB, "rsum", [P, 4])
        rinv = sb(sB, "rinv", [P, 4])
        o_low = sb(sB, "o_low", [DH, SEQ])
        o_sum = sb(sB, "o_sum", [DH, 2, SEQ])
        xn = sb(sB, "xn", [P, 2, EMBED])
        wo_raw = [w_raw[:, 0, :], w_raw[:, 1, :], w_raw[:, 2, :], xn[:, 0, :], xn[:, 1, :]]
        sB.close()

        sC = ExitStack()
        ar_hi = sb(sC, "ar_hi", [P, KC, ARW], F32R)
        ar_lo = sb(sC, "ar_lo", [P, KC, ARW], F32R)
        bt_hi = sb(sC, "bt_hi", [P, EMBED], F32R)
        bt_lo = sb(sC, "bt_lo", [P, EMBED], F32R)
        ar_raw = sb(sC, "ar_raw", [P, KC, ARW])
        bt_raw = sb(sC, "bt_raw", [P, EMBED])
        br_sb = sb(sC, "br_sb", [P, LOGITS])
        xres = sb(sC, "xres", [P, 2, EMBED])
        x1 = sb(sC, "x1", [P, 2, EMBED])
        z = sb(sC, "z", [P, EMBED])
        xn2 = sb(sC, "xn2", [P, EMBED])
        x2T_hi = sb(sC, "x2T_hi", [P, KC, P], F32R)
        x2T_lo = sb(sC, "x2T_lo", [P, KC, P], F32R)
        logit = sb(sC, "logit", [P, LOGITS])
        lmax = sb(sC, "lmax", [P, 1])
        lexp = sb(sC, "lexp", [P, LOGITS])
        lsum = sb(sC, "lsum", [P, 1])
        linv = sb(sC, "linv", [P, 1])
        score = sb(sC, "score", [P, LOGITS])
        wlow = sb(sC, "wlow", [P, HR])
        wlT_hi = sb(sC, "wlT_hi", [P, P], F32R)
        wlT_lo = sb(sC, "wlT_lo", [P, P], F32R)
        res = sb(sC, "res", [P, 2, EMBED])
        sC.close()

        tables_in = sem("tables_in")
        x_in = [sem(f"x_in{i}") for i in range(4)]
        w_in = [sem(f"w_in{m}") for m in range(3)]
        consts = sem("consts")
        ln_stat = sem("ln_stat")
        ln_dve = sem("ln_dve")
        ln_act = sem("ln_act")
        normed = sem("normed")
        tr_done = sem("tr_done")
        tr_hi = sem("tr_hi")
        tr_lo = sem("tr_lo")
        w_hi_done = [sem(f"w_hi_done{m}") for m in range(3)]
        w_lo_done = [sem(f"w_lo_done{m}") for m in range(3)]
        grp_done = sem("grp_done")
        grp_read = sem("grp_read")
        swap_done = sem("swap_done")
        rot_mul = sem("rot_mul")
        rot_done = sem("rot_done")
        qk_hi_done = sem("qk_hi_done")
        qk_lo_done = sem("qk_lo_done")
        s_done = sem("s_done")
        neg_done = sem("neg_done")
        exp_done = sem("exp_done")
        inv_done = sem("inv_done")
        prob_done = sem("prob_done")
        t_done = sem("t_done")
        pt_hi_done = sem("pt_hi_done")
        pt_lo_done = sem("pt_lo_done")
        pv_done = sem("pv_done")
        olow_done = sem("olow_done")
        osum_done = sem("osum_done")
        o_out = [sem(f"o_out{i}") for i in range(2)]
        wo_in = [sem(f"wo_in{i}") for i in range(5)]
        wo_hi_done = sem("wo_hi_done")
        wo_lo_done = [sem(f"wo_lo_done{i}") for i in range(2)]
        ffn_in = sem("ffn_in")
        ffn_hi_done = sem("ffn_hi_done")
        ffn_lo_done = sem("ffn_lo_done")
        oT_in = [sem(f"oT_in{i}") for i in range(2)]
        xres_in = [sem(f"xres_in{i}") for i in range(2)]
        oT_hi_done = sem("oT_hi_done")
        oT_lo_done = sem("oT_lo_done")
        y_done = sem("y_done")
        x1_done = sem("x1_done")
        x2t_done = sem("x2t_done")
        x2T_hi_done = sem("x2T_hi_done")
        x2T_lo_done = sem("x2T_lo_done")
        low_done = sem("low_done")
        soft_dve = sem("soft_dve")
        soft_exp = sem("soft_exp")
        wlow_done = sem("wlow_done")
        wlt_done = sem("wlt_done")
        wlT_hi_done = sem("wlT_hi_done")
        wlT_lo_done = sem("wlT_lo_done")
        e_done = sem("e_done")
        res_done = sem("res_done")
        out_out = [sem(f"out_out{i}") for i in range(2)]

        gate_dve = sem("gate_dve")
        gate_pool = sem("gate_pool")

        block = ctx.enter_context(nc.Block())

        def late(count, first):
            return not isinstance(count, int) or count >= first

        def real(u):
            return not isinstance(u, int) or 0 <= u < UNITS

        def trailing(u, s, lag):
            at = s - lag
            a, q = u - 1 + at // STEPS, at % STEPS
            return a, q, STEPS * a + q

        def x_fill(batch, c):
            v_before = {0: 0, 1: 0, 2: UPH - 2, 3: UPH - 1}[batch] + (1 if batch >= 2 and c >= 2 else 0)
            return CHUNKS * batch + c + v_before

        def v_fill(u, half):
            chunks = 2 * CHUNKS if half == 0 else 4 * CHUNKS
            if isinstance(u, int):
                chunks = {UPH - 1: 2 * CHUNKS + 2, UPH: 3 * CHUNKS + 2}.get(u, 2 * CHUNKS if u < UPH else 4 * CHUNKS)
            return u - 1 + chunks

        def x_turns(u, s):
            if not isinstance(u, int):
                return 0, [], []
            now = {0: 1, UPH - 1: 2, UPH: 3}.get(u)
            nxt = {UPH - 2: 2, UPH - 1: 3}.get(u)
            tiles = []
            if now is not None and s in (1, 3):
                tiles.append(4 * now + s // 2 + 2)
            if nxt == 2 and s in (3, 5):
                tiles.append(4 * nxt + s // 5)
            if nxt == 3 and s in (5, 7):
                tiles.append(4 * nxt + s // 7)
            return now, tiles, [s] if now is not None else []

        def x_ready(u, s):
            if s % 2 or not isinstance(u, int):
                return []
            return x_turns(u, s - 1)[1] if s else x_turns(u - 1, STEPS - 1)[1]

        def x_buffer(n):
            if n in (2, 3):
                return prob[:, 2 * n - 4:2 * n - 2, :].rearrange("p a b -> p (a b)"), x_in[n], 16
            return xin[:, n % 2, :], x_in[n % 2], 16 * (n // 2 + (1 if n < 2 else 0))

        def x_bank(batch, c):
            return bank[4 + c % 4] if batch == 0 else tr_ps

        def run_slots(eng, slot):
            for half in range(HALVES):
                slot(0, 0, half)
                slot(0, 1, half)
                with eng.Fori(1, PAIRS - 1) as pair:
                    slot(pair, 0, half)
                    slot(pair, 1, half)
                slot(PAIRS - 1, 0, half)
                slot(PAIRS - 1, 1, half)
            slot(PAIRS, 0, 1)
            slot(PAIRS, 1, 1)

        def tiled(t):
            return not isinstance(t, int) or 0 <= t < TILES

        def ln_first(t):
            return TILES + 3 * t - 1 if late(t, 2) else TILES + 2 * t

        def ln_second(t):
            return ln_first(t) + 1

        def ln_third(t):
            return 4 * TILES - 1 if isinstance(t, int) and t == TILES - 1 else TILES + 3 * t + 4

        @block.sync
        def _(sp):
            def load_x(n):
                if n >= 4:
                    sp.wait_ge(normed, n - 1 if n >= 6 else n - 3)
                dst, loaded, _ = x_buffer(n)
                sp.dma_start(dst, x[n * P:(n + 1) * P, :]).then_inc(loaded, 16)

            def load_w(m, n, pair):
                if late(n, 1):
                    sp.wait_ge(w_hi_done[m], n)
                    sp.wait_ge(w_lo_done[m], n)
                sp.dma_start(w_raw[:, m, :], wqkv[m, pair, :, :]).then_inc(w_in[m], 16)

            def store_o(u, pair, b, half, h):
                if real(u):
                    sp.wait_ge(osum_done, 2 * u + h + 1)
                    batch = 2 * half + b
                    sp.dma_start(scratch[2 * pair + h, :, batch * SEQ:(batch + 1) * SEQ],
                                 o_sum[:, h, :]).then_inc(o_out[h], 16)

            def load_wo(c):
                if c < 3:
                    sp.wait_ge(w_hi_done[c], 2 * PAIRS)
                    sp.wait_ge(w_lo_done[c], 2 * PAIRS)
                elif c == 3:
                    sp.wait_ge(tr_done, x_fill(3, CHUNKS - 1) + 1)
                elif c >= 5:
                    sp.wait_ge(wo_lo_done[(c - 5) % 2], (c - 5) // 2 + 1)
                sp.dma_start(wo_raw[c % 5], wo[c * P:(c + 1) * P, :]).then_inc(wo_in[c % 5], 16)

            def load_oT(t, i):
                if late(t, 2):
                    sp.wait_ge(oT_lo_done, t - 1)
                sp.dma_start(oT[:, i, :, :],
                             scratch.rearrange("(c h) d t -> (h d) c t", h=2)[:, :, bass.ds(t * P, P)]
                             ).then_inc(oT_in[i], 16)

            def load_xres(t, i):
                if late(t, 2):
                    sp.wait_ge(x1_done, t - 1)
                sp.dma_start(xres[:, i, :], x[bass.ds(t * P, P), :]).then_inc(xres_in[i], 16)

            load_x(0)
            load_x(1)
            load_w(0, 0, 0)
            load_x(2)
            load_x(3)
            sp.dma_start(cos_sb[:, :], cos).then_inc(tables_in, 16)
            sp.dma_start(sin_sb[:, :], sin).then_inc(tables_in, 16)
            load_w(1, 0, 0)
            load_w(2, 0, 0)
            for n in range(4, 6):
                load_x(n)

            def slot(pair, b, half):
                u = 2 * pair + b + UPH * half
                crossing = isinstance(pair, int) and pair == 0
                stored = (PAIRS - 1, half - 1) if crossing else (pair - 1, half)
                more = b == 0 and not (isinstance(u, int) and u >= UNITS - 2)
                n = pair + PAIRS * half + 1
                nxt = (pair + 1) % PAIRS if isinstance(pair, int) else pair + 1
                if more:
                    load_w(0, n, nxt)
                    load_w(1, n, nxt)
                if isinstance(u, int) and u == UNITS - 1:
                    for c in range(5):
                        load_wo(c)
                    sp.wait_ge(normed, TILES)
                    for h in range(2):
                        sp.wait_ge(o_out[h], 16 * UPH)
                    load_oT(0, 0)
                    load_oT(1, 1)
                if isinstance(u, int) and u == UNITS + 1:
                    load_oT(2, 0)
                    load_oT(3, 1)
                early = {0: (6,), UPH - 2: (8, 9), UPH - 1: (10,), UPH: (14,)}
                later = {0: (7,), UPH - 1: (11, 12, 13), UPH: (15,)}
                for t in early.get(u, ()) if isinstance(u, int) else ():
                    load_x(t)
                store_o(u - 2, stored[0], b, stored[1], 0)
                for t in later.get(u, ()) if isinstance(u, int) else ():
                    load_x(t)
                if more:
                    load_w(2, n, nxt)
                if isinstance(u, int) and u == UNITS:
                    for c in range(5, KC):
                        load_wo(c)
                store_o(u - 2, stored[0], b, stored[1], 1)

            run_slots(sp, slot)

            sp.wait_ge(pv_done, HEADS * BATCHES)
            for h in range(2):
                sp.wait_ge(o_out[h], 16 * UNITS)
            load_xres(0, 0)
            sp.dma_start(ar_raw[:, :, :], ar).then_inc(ffn_in, 16)
            sp.dma_start(bt_raw[:, :], bt).then_inc(ffn_in, 16)
            sp.dma_start(br_sb[:, :], br).then_inc(ffn_in, 16)
            load_xres(1, 1)

            def turn(t, i):
                more = tiled(t + 2) and not (isinstance(t, int) and t >= TILES - 2)
                if more and late(t, 2):
                    load_oT(t + 2, i)
                if tiled(t - 2):
                    sp.wait_ge(res_done, t - 1)
                    sp.dma_start(out[bass.ds((t - 2) * P, P), :], res[:, i, :]).then_inc(out_out[i], 16)
                if more:
                    load_xres(t + 2, i)

            turn(0, 0)
            turn(1, 1)
            with sp.Fori(2, TILES - 4, 2) as t:
                turn(t, 0)
                turn(t + 1, 1)
            for t in range(TILES - 4, TILES + 2):
                turn(t, t % 2)
            sp.wait_ge(out_out[0], 16 * TILES // 2)
            sp.wait_ge(out_out[1], 16 * TILES // 2)

        @block.gpsimd
        def _(pool):
            pool.memset(ident[:, :], 0.0).then_inc(consts, 1)
            pool.memset(mask[:, :], 0.0).then_inc(consts, 1)
            pool.wait_ge(consts, 2)
            pool.affine_select(out=ident[:, :], in_=ident[:, :], compare_op=ALU.not_equal, fill=1.0,
                               base=0, pattern=[[-1, P]], channel_multiplier=1).then_inc(consts, 1)
            diag = mask[:, SEQ - P:SEQ]
            pool.affine_select(out=diag, in_=diag, compare_op=ALU.is_ge, fill=MASKED,
                               base=0, pattern=[[-1, P]], channel_multiplier=1).then_inc(consts, 1)
            pool.wait_ge(tables_in, 32)

            def divide(u, s):
                a, q, g = trailing(u, s, 1)
                if real(a):
                    pool.wait_ge(inv_done, g + 1)
                    pool.sem_inc(gate_pool, 1)
                    p = prob[:, q % 4, 0:P * (q % QT + 1)]
                    pool.tensor_scalar(p, p, rinv[:, q % 4:q % 4 + 1], 1.0, ALU.mult, ALU.mult
                                       ).then_inc(prob_done, 1)

            def rotate(u, k):
                m = 2 * u + k
                pool.wait_ge(grp_read, 3 * u + k + 1)
                if late(m, 1):
                    pool.wait_ge(rot_done, m)
                    pool.wait_ge(qk_hi_done, 4 * u + 2 * k)
                    pool.wait_ge(qk_lo_done, 4 * u + 2 * k)
                pool.tensor_tensor(rot_c[:, :], raw[:, :], cos_sb[:, :], ALU.mult).then_inc(rot_mul, 1)
                pool.wait_ge(swap_done, m + 1)
                pool.tensor_tensor(swapped[:, :], swapped[:, :], sin_sb[:, :], ALU.mult).then_inc(rot_mul, 1)

            def w_low(m, n):
                pool.wait_ge(w_hi_done[m], n + 1)
                pool.tensor_tensor(w_lo[:, m, :], w_raw[:, m, :], w_hi[:, m, :].bitcast(F32), ALU.subtract
                                   ).then_inc(w_lo_done[m], 1)

            for m in range(3):
                w_low(m, 0)

            def slot(pair, b, half):
                u = 2 * pair + b + UPH * half
                n = pair + PAIRS * half
                for s in range(STEPS):
                    if real(u) and s in (3, 6):
                        rotate(u, s // 6)
                    divide(u, s)
                    if s == 1 and b == 0 and real(u) and late(n, 1):
                        w_low(2, n)
                    if s in (4, 7) and b == 1 and not (isinstance(u, int) and u >= UNITS - 1):
                        w_low(s // 7, n + 1)
                    if isinstance(u, int) and u == UNITS - 1 and s in (4, 7):
                        oT_low(s // 7, s // 7)
                    if isinstance(u, int) and u == UNITS and s % 2:
                        pool.wait_ge(wo_hi_done, s + 1)
                        pool.tensor_tensor(wo_lo[:, s, :], wo_raw[s % 5], wo_hi[:, s, :].bitcast(F32), ALU.subtract
                                           ).then_inc(wo_lo_done[1], 1)

            def oT_low(t, i):
                pool.wait_ge(oT_hi_done, t + 1)
                pool.tensor_tensor(oT_lo[:, i, :, :], oT[:, i, :, :], oT_hi[:, i, :, :].bitcast(F32), ALU.subtract
                                   ).then_inc(oT_lo_done, 1)

            run_slots(pool, slot)


            def turn(t, i):
                if tiled(t - 2):
                    pool.wait_ge(normed, ln_third(t - 2) + 1)
                    pool.tensor_tensor(res[:, i, :], res[:, i, :], x1[:, i, :], ALU.add).then_inc(res_done, 1)
                if tiled(t + 2) and not (isinstance(t, int) and t >= TILES - 2):
                    oT_low(t + 2, i)

            turn(0, 0)
            turn(1, 1)
            turn(2, 0)
            turn(3, 1)
            with pool.Fori(4, TILES - 2, 2) as t:
                turn(t, 0)
                turn(t + 1, 1)
            for t in range(TILES - 2, TILES + 2):
                turn(t, t % 2)

        @block.scalar
        def _(act):
            def ln_start(n):
                act.wait_ge(ln_dve, LN_STEPS * n + 1)
                act.activation(lnv[:, :], ve[:, :], ACT.Ln).then_inc(ln_act, 1)
                act.wait_ge(ln_act, 2 * n + 1)
                act.activation(r0[:, :], lnv[:, :], ACT.Exp, scale=-0.5).then_inc(ln_act, 1)

            def ln_rstd(n):
                ln_start(n)
                act.wait_ge(ln_dve, LN_STEPS * n + LN_STEPS)

            def normal(dst, src):
                return act.activation(dst, src, ACT.Identity, bias=nmr[:, 0:1], scale=rstd[:, 0:1])

            def x_normal(n):
                act.wait_ge(ln_dve, LN_STEPS * (n + 1))
                if n >= 2:
                    act.wait_ge(tr_done, x_fill((n - 2) // 4, 2 * ((n - 2) % 4) + 1) + 1)
                normal(xn[:, n % 2, :], x_buffer(n)[0]).then_inc(normed, 1)

            def x_chunk(batch, c):
                act.wait_ge(tr_done, x_fill(batch, c) + 1)
                if batch >= 2 and c == 0:
                    act.wait_ge(grp_done, 3 * (UPH - 3 + batch))
                dst = xT_hi[:, batch % 2, 4 * (c % 2):4 * (c % 2) + 4, P * (c // 2):P * (c // 2) + P]
                act.activation(dst, x_bank(batch, c)[:, :].rearrange("p (c t) -> p c t", c=4), ACT.Copy).then_inc(tr_hi, 1)

            def w_high(m, n):
                act.wait_ge(w_in[m], 16 * n + 16)
                if late(n, 1):
                    act.wait_ge(grp_done, 6 * n - 2 + m)
                act.activation(w_hi[:, m, :], w_raw[:, m, :], ACT.Copy).then_inc(w_hi_done[m], 1)

            def exponent(u, s):
                a, q, g = trailing(u, s, 1)
                if real(a):
                    n = P * (q % QT + 1)
                    act.wait_ge(neg_done, g + 1)
                    if late(g, 4):
                        act.wait_ge(t_done, g - 3)
                    act.activation(prob[:, q % 4, 0:n], neg[:, q % 2, 0:n], ACT.Exp, scale=-1.0,
                                   bias=nmax[:, q % 4:q % 4 + 1], accum_out=rsum[:, q % 4:q % 4 + 1]
                                   ).then_inc(exp_done, 1)

            def pt_high(u, s):
                a, q, g = trailing(u, s, 3)
                if real(a):
                    i, h = q % QT, q // QT
                    act.wait_ge(t_done, g + 1)
                    if late(a, 1):
                        act.wait_ge(pv_done, 2 * a + h - 1)
                    act.activation(pT_hi[:, h, 0:i + 1, P * i:P * i + P],
                                   pt_ps[q % 2][:, 0:P * (i + 1)].rearrange("p (j t) -> p j t", j=i + 1),
                                   ACT.Copy).then_inc(pt_hi_done, 1)

            def qk_raw(u, b, k, fill):
                m = 2 * u + k
                act.wait_ge(grp_done, 3 * u + k + 1)
                if k == 1:
                    act.wait_ge(rot_done, m)
                elif late(u, 1):
                    act.wait_ge(tr_done, fill + 1)
                act.activation(raw[:, :], grp_ps[(b + k) % 2][:, :], ACT.Copy).then_inc(grp_read, 1)

            def q_high(u, b):
                act.wait_ge(rot_done, 2 * u + 1)
                if late(u, 2):
                    act.wait_ge(s_done, STEPS * (u - 1))
                for h in range(2):
                    own = slice(DH * h, DH * h + DH)
                    act.activation(q_hl[own, b, h, :], rot_c[own, :], ACT.Copy).then_inc(qk_hi_done, 1)

            def k_high(u, b, h):
                own = slice(DH * h, DH * h + DH)
                act.wait_ge(rot_done, 2 * u + 2)
                act.activation(k_hh[own, b, h, :], rot_c[own, :], ACT.Copy).then_inc(qk_hi_done, 1)

            def v_raw(u, b):
                act.wait_ge(grp_done, 3 * u + 3)
                act.wait_ge(rot_done, 2 * u + 2)
                act.activation(raw[:, :], grp_ps[b][:, :], ACT.Copy).then_inc(grp_read, 1)

            def v_high(u, b, fill):
                act.wait_ge(tr_done, fill + 1)
                if late(u, 2):
                    act.wait_ge(pv_done, 2 * (u - 1))
                act.activation(v_hl[:, b, :, :, 0:DH].rearrange("p j h d -> p (j h) d"),
                               tr_ps[:, :].rearrange("p (j d) -> p j d", d=DH), ACT.Copy).then_inc(tr_hi, 1)

            def o_lower(a, h):
                n = 2 * a + h
                act.wait_ge(pv_done, n + 1)
                if late(n, 1):
                    act.wait_ge(osum_done, n)
                act.activation(o_low[:, :], o_ps[DH:2 * DH, :], ACT.Copy).then_inc(olow_done, 1)

            def slot(pair, b, half):
                u = 2 * pair + b + UPH * half
                n = pair + PAIRS * half
                fill = v_fill(u, half)
                for s in range(STEPS):
                    batch, tiles, chunks = x_turns(u, s)
                    if s == 3 and real(u):
                        qk_raw(u, b, 0, fill)
                    exponent(u, s)
                    if real(u):
                        if s == 4:
                            q_high(u, b)
                        if s == 7:
                            k_high(u, b, 0)
                    if s == 0 and real(u - 1):
                        v_raw(u - 1, 1 - b)
                    if s == 1 and real(u - 2):
                        o_lower(u - 2, 0)
                    if s == 5 and real(u - 2):
                        o_lower(u - 2, 1)
                    if s == 2 and real(u - 1):
                        v_high(u - 1, 1 - b, fill)
                    for t in x_ready(u, s):
                        ln_start(t)
                    pt_high(u, s)
                    if real(u):
                        if s == 0 and b == 0 and late(n, 1):
                            w_high(2, n)
                        if s == 5:
                            qk_raw(u, b, 1, fill)
                        if s == 7:
                            k_high(u, b, 1)
                        if b == 1 and not (isinstance(u, int) and u == UNITS - 1):
                            if s == 3:
                                w_high(0, n + 1)
                            if s == 6:
                                w_high(1, n + 1)
                    for c in chunks:
                        x_chunk(batch, c)
                    for t in x_ready(u, s):
                        x_normal(t)
                    if isinstance(u, int) and u == UNITS - 1 and s in (3, 6):
                        act.wait_ge(grp_done, 3 * u + s // 3)
                        oT_high(s // 6, s // 6, 16)
                    if isinstance(u, int) and u == UNITS:
                        if s == 0:
                            act.wait_ge(grp_done, 3 * UNITS)
                        wo_high(s)
                    if isinstance(u, int) and u == UNITS + 1 and s == 5:
                        ln_start(ln_first(0))

            def wo_high(c):
                act.wait_ge(wo_in[c % 5], 16 * (c // 5 + 1))
                act.activation(wo_hi[:, c, :], wo_raw[c % 5], ACT.Copy).then_inc(wo_hi_done, 1)

            def oT_high(t, i, count):
                act.wait_ge(oT_in[i], count)
                if late(t, 2):
                    act.wait_ge(y_done, t - 1)
                act.activation(oT_hi[:, i, :, :], oT[:, i, :, :], ACT.Copy).then_inc(oT_hi_done, 1)

            act.preload_act_table_set("natural_log_exp_and_others")
            for n in range(6):
                ln_start(n)
                if 1 <= n <= 4:
                    x_chunk(0, 2 * n - 2)
                    x_chunk(0, 2 * n - 1)
                x_normal(n)
                if n in (0, 3, 4):
                    w_high(max(0, n - 2), 0)
            run_slots(act, slot)

            def x2T_high(t, k):
                act.wait_ge(x2t_done, 2 * t + k + 1)
                if late(t, 1) and k == 0:
                    act.wait_ge(low_done, t)
                act.activation(x2T_hi[:, 4 * k:4 * k + 4, :], tr_ps[:, :].rearrange("p (c t) -> p c t", c=4),
                               ACT.Copy).then_inc(x2T_hi_done, 1)

            def turn(t, i):
                if tiled(t - 2):
                    ln_start(ln_third(t - 2))
                middle = tiled(t - 1) and not (isinstance(t, int) and t > TILES)
                if middle:
                    x2T_high(t - 1, 0)
                if tiled(t - 2):
                    act.wait_ge(ln_dve, LN_STEPS * (ln_third(t - 2) + 1))
                    if late(t, 4):
                        act.wait_ge(out_out[i], 8 * (t - i) - 16)
                    for k in range(2):
                        done = normal(res[:, i, 512 * k:512 * k + 512], pt_ps[k][:, :])
                    done.then_inc(normed, 1)
                if middle:
                    x2T_high(t - 1, 1)
                if tiled(t) and late(t, 1):
                    ln_start(ln_first(t))
                if middle:
                    act.wait_ge(soft_dve, 5 * (t - 1) + 2)
                    act.activation(lexp[:, :], logit[:, :], ACT.Exp, bias=lmax[:, 0:1],
                                   accum_out=lsum[:, 0:1]).then_inc(soft_exp, 1)
                if tiled(t):
                    act.wait_ge(ln_dve, LN_STEPS * (ln_first(t) + 1))
                    if isinstance(t, int) and t == 0:
                        act.wait_ge(pv_done, HEADS * BATCHES)
                        act.wait_ge(osum_done, HEADS * BATCHES)
                    for k in range(2):
                        done = normal(z[:, 512 * k:512 * k + 512], y_ps[i][k][:, :])
                    done.then_inc(normed, 1)
                if tiled(t + 2) and not (isinstance(t, int) and t >= TILES - 2):
                    oT_high(t + 2, i, 8 * (t + 2 - i) + 16)
                if middle:
                    act.wait_ge(wlt_done, t)
                    if late(t, 2):
                        act.wait_ge(e_done, t - 1)
                    act.activation(wlT_hi[:, :], o_ps[:, WLT:WLT + P], ACT.Copy).then_inc(wlT_hi_done, 1)
                if tiled(t):
                    ln_rstd(ln_second(t))
                    normal(xn2[:, :], x1[:, i, :]).then_inc(normed, 1)
                if isinstance(t, int) and t == 0:
                    act.wait_ge(ffn_in, 48)
                    act.activation(ar_hi[:, :, :], ar_raw[:, :, :], ACT.Copy).then_inc(ffn_hi_done, 1)
                    act.activation(bt_hi[:, :], bt_raw[:, :], ACT.Copy).then_inc(ffn_hi_done, 1)

            turn(0, 0)
            turn(1, 1)
            turn(2, 0)
            turn(3, 1)
            with act.Fori(4, TILES - 2, 2) as t:
                turn(t, 0)
                turn(t + 1, 1)
            for t in range(TILES - 2, TILES + 2):
                turn(t, t % 2)

        @block.vector
        def _(dve):
            def ln_stats(src):
                dve.bn_stats(stats[:, 0, :], src[0]).then_inc(ln_stat, 1)
                dve.bn_stats(stats[:, 1, :], src[1]).then_inc(ln_stat, 1)

            def layernorm(n, src):
                ln_stats(src)
                ln_variance(n)
                ln_scale(n)

            def ln_variance(n):
                dve.wait_ge(ln_stat, 3 * n + 2)
                dve.sem_inc(gate_dve, 1)
                dve.bn_aggr(mv[:, :], stats[:, :, :].rearrange("p a b -> p (a b)")).then_inc(ln_stat, 1)
                dve.wait_ge(ln_stat, 3 * n + 3)
                dve.tensor_scalar(ve[:, :], mv[:, 1:2], EPS, None, ALU.add).then_inc(ln_dve, 1)

            def ln_scale(n):
                dve.wait_ge(ln_act, 2 * n + 2)
                dve.wait_ge(ln_dve, LN_STEPS * n + 1)
                dve.scalar_tensor_tensor(out=rr[:, :], in0=r0[:, :], scalar=ve[:, 0:1], in1=r0[:, :],
                                         op0=ALU.mult, op1=ALU.mult).then_inc(ln_dve, 1)
                dve.wait_ge(ln_dve, LN_STEPS * n + 2)
                dve.tensor_scalar(cc[:, :], rr[:, :], -0.5, 1.5, ALU.mult, ALU.add).then_inc(ln_dve, 1)
                if late(n, 1):
                    dve.wait_ge(normed, n)
                dve.wait_ge(ln_dve, LN_STEPS * n + 3)
                dve.tensor_tensor(rstd[:, :], cc[:, :], r0[:, :], ALU.mult).then_inc(ln_dve, 1)
                dve.wait_ge(ln_dve, LN_STEPS * n + 4)
                dve.scalar_tensor_tensor(out=nmr[:, :], in0=mv[:, 0:1], scalar=-1.0, in1=rstd[:, :],
                                         op0=ALU.mult, op1=ALU.mult).then_inc(ln_dve, 1)

            def x_stats(n):
                tile, loaded, count = x_buffer(n)
                dve.wait_ge(loaded, count)
                ln_stats([tile[:, 0:512], tile[:, 512:1024]])

            def x_variance(n):
                x_stats(n)
                ln_variance(n)

            def x_chunk(batch, c):
                dve.wait_ge(tr_hi, x_fill(batch, c) + 1)
                at = (slice(None), batch % 2, slice(4 * (c % 2), 4 * (c % 2) + 4),
                      slice(P * (c // 2), P * (c // 2) + P))
                dve.tensor_tensor(xT_lo[at], x_bank(batch, c)[:, :].rearrange("p (c t) -> p c t", c=4),
                                  xT_hi[at].bitcast(F32), ALU.subtract).then_inc(tr_lo, 1)

            def negate(u, s):
                a, q, g = trailing(u, s, 1)
                if real(a):
                    n = P * (q % QT + 1)
                    dve.wait_ge(s_done, g + 1)
                    if late(g, 2):
                        dve.wait_ge(exp_done, g - 1)
                    dve.sem_inc(gate_dve, 1)
                    dve.tensor_tensor_reduce(neg[:, q % 2, 0:n], sc_ps[q % 2][:, 0:n], mask[:, SEQ - n:SEQ],
                                             -SOFT, 3e38, ALU.add, ALU.min, nmax[:, q % 4:q % 4 + 1]
                                             ).then_inc(neg_done, 1)

            def invert(u, s):
                a, q, g = trailing(u, s, 1)
                if real(a):
                    dve.wait_ge(exp_done, g + 1)
                    if late(g, 4):
                        dve.wait_ge(prob_done, g - 3)
                    dve.reciprocal(rinv[:, q % 4:q % 4 + 1], rsum[:, q % 4:q % 4 + 1]).then_inc(inv_done, 1)

            def pt_low(u, s):
                a, q, g = trailing(u, s, 3)
                if real(a):
                    i, h = q % QT, q // QT
                    dve.wait_ge(pt_hi_done, g + 1)
                    at = (slice(None), h, slice(0, i + 1), slice(P * i, P * i + P))
                    dve.tensor_tensor(pT_lo[at], pt_ps[q % 2][:, 0:P * (i + 1)].rearrange("p (j t) -> p j t", j=i + 1),
                                      pT_hi[at].bitcast(F32), ALU.subtract).then_inc(pt_lo_done, 1)

            def swap(u, k):
                m = 2 * u + k
                dve.wait_ge(grp_read, 3 * u + k + 1)
                if late(m, 1):
                    dve.wait_ge(rot_mul, 2 * m)
                dve.sem_inc(gate_dve, 1)
                dve.stream_shuffle(swapped[:, :], raw[:, :], SWAP).then_inc(swap_done, 1)

            def rotate(u, k):
                m = 2 * u + k
                dve.wait_ge(rot_mul, 2 * m + 2)
                dve.tensor_tensor(rot_c[:, :], rot_c[:, :], swapped[:, :], ALU.add).then_inc(rot_done, 1)

            def q_low(u, b, h):
                own, other = slice(DH * h, DH * h + DH), slice(DH * (1 - h), DH * (1 - h) + DH)
                dve.wait_ge(qk_hi_done, 4 * u + 1 + h)
                dve.tensor_tensor(q_hl[other, b, h, :], rot_c[own, :], q_hl[own, b, h, :].bitcast(F32),
                                  ALU.subtract).then_inc(qk_lo_done, 1)

            def k_low(u, b, h):
                own, other = slice(DH * h, DH * h + DH), slice(DH * (1 - h), DH * (1 - h) + DH)
                dve.wait_ge(qk_hi_done, 4 * u + 3 + h)
                dve.tensor_tensor(k_lo[own, b, :], rot_c[own, :], k_hh[own, b, h, :].bitcast(F32), ALU.subtract)
                dve.tensor_copy(k_hh[other, b, h, :], k_hh[own, b, h, :]).then_inc(qk_lo_done, 1)

            def v_low(b, fill):
                dve.wait_ge(tr_hi, fill + 1)
                dve.tensor_tensor(v_hl[:, b, :, :, DH:2 * DH].rearrange("p j h d -> p (j h) d"),
                                  tr_ps[:, :].rearrange("p (j d) -> p j d", d=DH),
                                  v_hl[:, b, :, :, 0:DH].rearrange("p j h d -> p (j h) d").bitcast(F32),
                                  ALU.subtract).then_inc(tr_lo, 1)

            def o_add(a, h):
                dve.wait_ge(olow_done, 2 * a + h + 1)
                if late(a, 1):
                    dve.wait_ge(o_out[h], 16 * a)
                dve.tensor_tensor(o_sum[:, h, :], o_ps[0:DH, :], o_low[:, :], ALU.add).then_inc(osum_done, 1)

            def slot(pair, b, half):
                u = 2 * pair + b + UPH * half
                fill = v_fill(u, half)
                for s in range(STEPS):
                    batch, tiles, chunks = x_turns(u, s)
                    negate(u, s)
                    if real(u):
                        if s in (3, 6):
                            swap(u, s // 6)
                        if s in (4, 7):
                            rotate(u, s // 7)
                    if s == 1 and real(u - 2):
                        o_add(u - 2, 0)
                    if s == 6 and real(u - 2):
                        o_add(u - 2, 1)
                    invert(u, s)
                    if s == 2 and real(u - 1):
                        v_low(1 - b, fill)
                    pt_low(u, s)
                    if s == 0 and real(u - 1):
                        k_low(u - 1, 1 - b, 1)
                    if real(u):
                        if s in (4, 5):
                            q_low(u, b, s - 4)
                        if s == 7:
                            k_low(u, b, 0)
                    for t in x_ready(u, s):
                        ln_scale(t)
                    for t in tiles:
                        x_variance(t)
                    for c in chunks:
                        x_chunk(batch, c)
                    if isinstance(u, int) and u == UNITS and s % 2 == 0:
                        dve.wait_ge(wo_hi_done, s + 1)
                        dve.tensor_tensor(wo_lo[:, s, :], wo_raw[s % 5], wo_hi[:, s, :].bitcast(F32), ALU.subtract
                                          ).then_inc(wo_lo_done[0], 1)
                    if isinstance(u, int) and u == UNITS + 1 and s == 5:
                        y_variance(0, 0)

            def y_variance(t, i):
                dve.wait_ge(y_done, t + 1)
                ln_stats([y[:, :] for y in y_ps[i]])
                ln_variance(ln_first(t))

            dve.wait_ge(consts, 4)
            x_variance(0)
            x_stats(1)
            for n in range(6):
                ln_scale(n)
                if n < 5:
                    dve.wait_ge(ln_dve, LN_STEPS * (n + 1))
                    ln_variance(n + 1)
                if 1 <= n <= 4:
                    x_chunk(0, 2 * n - 2)
                    x_chunk(0, 2 * n - 1)
                if n < 4:
                    x_stats(n + 2)
            run_slots(dve, slot)

            def turn(t, i):
                middle = tiled(t - 1) and not (isinstance(t, int) and t > TILES)
                if tiled(t - 2):
                    dve.wait_ge(e_done, t - 1)
                    layernorm(ln_third(t - 2), [e[:, :] for e in pt_ps])
                if middle:
                    for k in range(2):
                        dve.wait_ge(x2T_hi_done, 2 * (t - 1) + k + 1)
                        dve.tensor_tensor(x2T_lo[:, 4 * k:4 * k + 4, :],
                                          tr_ps[:, :].rearrange("p (c t) -> p c t", c=4),
                                          x2T_hi[:, 4 * k:4 * k + 4, :].bitcast(F32), ALU.subtract
                                          ).then_inc(x2T_lo_done, 1)
                if tiled(t) and late(t, 1):
                    y_variance(t, i)
                if middle:
                    m = 5 * (t - 1)
                    dve.wait_ge(low_done, t)
                    dve.tensor_tensor(logit[:, :], o_ps[:, HR:ARW], br_sb[:, :], ALU.add).then_inc(soft_dve, 1)
                    dve.wait_ge(soft_dve, m + 1)
                    dve.tensor_reduce(lmax[:, :], logit[:, :], AX.X, ALU.max, negate=True).then_inc(soft_dve, 1)
                if tiled(t):
                    ln_scale(ln_first(t))
                if middle:
                    dve.wait_ge(soft_exp, t)
                    dve.reciprocal(linv[:, :], lsum[:, :]).then_inc(soft_dve, 1)
                    dve.wait_ge(soft_dve, m + 3)
                    dve.tensor_scalar(score[:, :], lexp[:, :], linv[:, 0:1], SCORE_SCALE, ALU.mult, ALU.mult
                                      ).then_inc(soft_dve, 2)
                    dve.wait_ge(soft_dve, m + 5)
                    if late(t, 2):
                        dve.wait_ge(wlt_done, t - 1)
                    dve.tensor_tensor(wlow[:, :].rearrange("p (h r) -> p h r", h=EXPERTS),
                                      o_ps[:, 0:HR].rearrange("p (h r) -> p h r", h=EXPERTS),
                                      score[:, :].rearrange("p (h o) -> p h o", o=1).to_broadcast([P, EXPERTS, RANK]),
                                      ALU.mult).then_inc(wlow_done, 1)
                if tiled(t):
                    dve.wait_ge(normed, ln_first(t) + 1)
                    dve.wait_ge(xres_in[i], 8 * (t - i) + 16)
                    if late(t, 2):
                        dve.wait_ge(res_done, t - 1)
                    if isinstance(t, int) and t == 0:
                        dve.wait_ge(pv_done, HEADS * BATCHES)
                        for h in range(2):
                            dve.wait_ge(o_out[h], 16 * UNITS)
                    dve.tensor_tensor(x1[:, i, :], z[:, :], xres[:, i, :], ALU.add).then_inc(x1_done, 1)
                if middle:
                    dve.wait_ge(wlT_hi_done, t)
                    dve.tensor_tensor(wlT_lo[:, :], o_ps[:, WLT:WLT + P], wlT_hi[:, :].bitcast(F32), ALU.subtract
                                      ).then_inc(wlT_lo_done, 1)
                if tiled(t):
                    dve.wait_ge(x1_done, t + 1)
                    layernorm(ln_second(t), [x1[:, i, 0:512], x1[:, i, 512:1024]])
                if isinstance(t, int) and t == 0:
                    dve.wait_ge(ffn_hi_done, 2)
                    dve.tensor_tensor(ar_lo[:, :, :], ar_raw[:, :, :], ar_hi[:, :, :].bitcast(F32), ALU.subtract
                                      ).then_inc(ffn_lo_done, 1)
                    dve.tensor_tensor(bt_lo[:, :], bt_raw[:, :], bt_hi[:, :].bitcast(F32), ALU.subtract
                                      ).then_inc(ffn_lo_done, 1)

            turn(0, 0)
            turn(1, 1)
            turn(2, 0)
            turn(3, 1)
            with dve.Fori(4, TILES - 2, 2) as t:
                turn(t, 0)
                turn(t + 1, 1)
            for t in range(TILES - 2, TILES + 2):
                turn(t, t % 2)

        @block.tensor
        def _(pe):
            def products(dst, terms, first, last):
                for n, (lhsT, rhs) in enumerate(terms):
                    mm = pe.matmul(dst, lhsT, rhs, start=first and n == 0, stop=last and n == len(terms) - 1)
                return mm

            def x_chunk(batch, c):
                f = x_fill(batch, c)
                pe.wait_ge(normed, 4 * batch + c // 2 + 1)
                reads = f if batch else c - 3
                if reads > 0:
                    pe.wait_ge(tr_hi, reads)
                    pe.wait_ge(tr_lo, reads)
                for k in range(4):
                    col = P * (4 * (c % 2) + k)
                    last = pe.transpose(x_bank(batch, c)[:, P * k:P * k + P], xn[:, c // 2 % 2, col:col + P], ident[:, :])
                last.then_inc(tr_done, 1)

            def v_turn(u, fill):
                pe.wait_ge(grp_read, 3 * u + 3)
                pe.wait_ge(tr_hi, fill)
                pe.wait_ge(tr_lo, fill)
                for k in range(QT):
                    last = pe.transpose(tr_ps[:, P * k:P * k + P], raw[:, P * k:P * k + P], ident[:, :])
                last.then_inc(tr_done, 1)

            def project(u, b, n, half, first, count):
                for mm in range(first, first + count):
                    k, at = mm // GROUP_MM, mm % GROUP_MM
                    c, part = at // 3, at % 3
                    if at == 0:
                        pe.wait_ge(w_hi_done[k], n + 1)
                        pe.wait_ge(w_lo_done[k], n + 1)
                        if late(3 * u + k, 2):
                            pe.wait_ge(grp_read, 3 * u + k - 1)
                        if isinstance(u, int) and u in (0, 1, UPH, UPH + 1) and k == 0:
                            f = x_fill(2 * half + b, CHUNKS - 1) + 1
                            pe.wait_ge(tr_hi, f)
                            pe.wait_ge(tr_lo, f)
                    w = (w_lo if part == 2 else w_hi)[:, k, P * c:P * c + P]
                    xt = (xT_lo if part == 1 else xT_hi)[:, b, c, :]
                    done = pe.matmul(grp_ps[(b + k) % 2][:, :], w, xt, start=at == 0, stop=at == GROUP_MM - 1)
                    if at == GROUP_MM - 1:
                        done.then_inc(grp_done, 1)

            def scores(u, s, b):
                a, q, g = trailing(u, s, 1)
                if real(a):
                    ab = (b + 1 + (s - 1) // STEPS) % 2
                    i, h = q % QT, q // QT
                    if q % QT == 0:
                        pe.wait_ge(qk_lo_done, 4 * a + 3 + h)
                        pe.wait_ge(qk_hi_done, 4 * a + 3 + h)
                    if late(g, 2):
                        pe.wait_ge(neg_done, g - 1)
                    own = slice(DH * h, DH * h + DH)
                    qc, kc = slice(P * i, P * i + P), slice(0, P * i + P)
                    products(sc_ps[q % 2][:, kc], [(q_hl[:, ab, h, qc], k_hh[:, ab, h, kc]),
                                                   (q_hl[own, ab, h, qc], k_lo[own, ab, kc])], True, True
                             ).then_inc(s_done, 1)

            def turn_probs(u, s):
                a, q, g = trailing(u, s, 3)
                if real(a):
                    pe.wait_ge(prob_done, g + 1)
                    if late(g, 2):
                        pe.wait_ge(pt_hi_done, g - 1)
                        pe.wait_ge(pt_lo_done, g - 1)
                    for j in range(q % QT + 1):
                        last = pe.transpose(pt_ps[q % 2][:, P * j:P * j + P], prob[:, q % 4, P * j:P * j + P],
                                            ident[:, :])
                    last.then_inc(t_done, 1)

            def attend(a, b, h, fill):
                if real(a):
                    g = STEPS * a + QT * h + QT - 1
                    pe.wait_ge(pt_hi_done, g + 1)
                    pe.wait_ge(pt_lo_done, g + 1)
                    if h == 0:
                        pe.wait_ge(tr_hi, fill)
                        pe.wait_ge(tr_lo, fill)
                    if late(2 * a + h, 1):
                        pe.wait_ge(osum_done, 2 * a + h)
                    for j in range(QT):
                        cols = slice(P * j, SEQ)
                        v = v_hl[:, b, j, h, :]
                        last = products(o_ps[:, cols], [(v, pT_hi[:, h, j, cols]), (v, pT_lo[:, h, j, cols])],
                                        j == 0, j == QT - 1)
                    last.then_inc(pv_done, 1)

            def y_half(t, i, k, c0, c1):
                if k == 0 and c0 == 0:
                    if isinstance(t, int) and t == 0:
                        pe.wait_ge(grp_read, 3 * UNITS)
                    pe.wait_ge(oT_hi_done, t + 1)
                    pe.wait_ge(oT_lo_done, t + 1)
                    if late(t, 2):
                        pe.wait_ge(normed, ln_first(t - 2) + 1)
                for c in range(c0, c1):
                    if isinstance(t, int) and t == 0 and k == 0:
                        pe.wait_ge(wo_hi_done, c + 1)
                        pe.wait_ge(wo_lo_done[c % 2], c // 2 + 1)
                    cols = slice(512 * k, 512 * k + 512)
                    last = products(y_ps[i][k][:, :], [(oT_hi[:, i, c, :], wo_hi[:, c, cols]),
                                                       (oT_lo[:, i, c, :], wo_hi[:, c, cols]),
                                                       (oT_hi[:, i, c, :], wo_lo[:, c, cols])], c == 0, c == KC - 1)
                if k == 1 and c1 == KC:
                    last.then_inc(y_done, 1)

            def slot(pair, b, half):
                u = 2 * pair + b + UPH * half
                n = pair + PAIRS * half
                fill = v_fill(u, half)
                for s in range(STEPS):
                    third = MM_STEP // 3

                    def project_third(k):
                        if real(u):
                            project(u, b, n, half, MM_STEP * s + third * k, third)

                    project_third(0)
                    if s == 2 and real(u - 1):
                        v_turn(u - 1, fill)
                    scores(u, s, b)
                    project_third(1)
                    turn_probs(u, s)
                    project_third(2)
                    if s == 0:
                        attend(u - 2, b, 0, v_fill(u - 1, half) + 1)
                    if s == 4:
                        attend(u - 2, b, 1, None)
                    batch, _, chunks = x_turns(u, s)
                    for c in chunks:
                        x_chunk(batch, c)
                    if isinstance(u, int) and STEPS * u + s in range(STEPS * UNITS + 2, STEPS * UNITS + KC + 2):
                        c = STEPS * (u - UNITS) + s - 2
                        y_half(0, 0, 0, c, c + 1)
                        y_half(0, 0, 1, c, c + 1)

            pe.wait_ge(consts, 4)
            for c in range(CHUNKS):
                x_chunk(0, c)
            run_slots(pe, slot)

            pe.wait_ge(neg_done, STEPS * UNITS)
            pe.wait_ge(osum_done, HEADS * BATCHES)

            def x2_turn(t, k):
                if k == 0:
                    pe.wait_ge(normed, ln_second(t) + 1)
                if late(2 * t + k, 1):
                    pe.wait_ge(x2T_hi_done, 2 * t + k)
                    pe.wait_ge(x2T_lo_done, 2 * t + k)
                for c in range(4):
                    last = pe.transpose(tr_ps[:, P * c:P * c + P], xn2[:, P * (4 * k + c):P * (4 * k + c) + P],
                                        ident[:, :])
                last.then_inc(x2t_done, 1)

            def low_rank(t):
                if isinstance(t, int) and t == 0:
                    pe.wait_ge(ffn_lo_done, 2)
                if late(t, 1):
                    pe.wait_ge(wlT_hi_done, t)
                    pe.wait_ge(wlT_lo_done, t)
                for c in range(KC):
                    if c % 4 == 0:
                        pe.wait_ge(x2T_hi_done, 2 * t + c // 4 + 1)
                        pe.wait_ge(x2T_lo_done, 2 * t + c // 4 + 1)
                    last = products(o_ps[:, 0:ARW], [(x2T_hi[:, c, :], ar_hi[:, c, :]), (x2T_lo[:, c, :], ar_hi[:, c, :]),
                                                     (x2T_hi[:, c, :], ar_lo[:, c, :])], c == 0, c == KC - 1)
                last.then_inc(low_done, 1)

            def experts(t):
                pe.wait_ge(wlT_hi_done, t + 1)
                pe.wait_ge(wlT_lo_done, t + 1)
                if late(t, 1):
                    pe.wait_ge(normed, ln_third(t - 1) + 1)
                for k in range(2):
                    cols = slice(512 * k, 512 * k + 512)
                    last = products(pt_ps[k][:, :], [(wlT_hi[:, :], bt_hi[:, cols]), (wlT_lo[:, :], bt_hi[:, cols]),
                                                     (wlT_hi[:, :], bt_lo[:, cols])], True, True)
                last.then_inc(e_done, 1)

            def turn(t, i):
                running = tiled(t) and not (isinstance(t, int) and t == 0)
                middle = tiled(t - 1) and not (isinstance(t, int) and t > TILES)
                if running:
                    y_half(t, i, 0, 0, 5)
                if tiled(t - 2):
                    pe.wait_ge(wlow_done, t - 1)
                    pe.transpose(o_ps[:, WLT:WLT + P], wlow[:, :], ident[:, :]).then_inc(wlt_done, 1)
                if running:
                    y_half(t, i, 0, 5, KC)
                if tiled(t - 2):
                    experts(t - 2)
                if running:
                    y_half(t, i, 1, 0, 4)
                if middle:
                    x2_turn(t - 1, 0)
                if running:
                    y_half(t, i, 1, 4, 7)
                if middle:
                    x2_turn(t - 1, 1)
                if running:
                    y_half(t, i, 1, 7, KC)
                if middle:
                    low_rank(t - 1)

            turn(0, 0)
            turn(1, 1)
            turn(2, 0)
            turn(3, 1)
            with pe.Fori(4, TILES - 2, 2) as t:
                turn(t, 0)
                turn(t + 1, 1)
            for t in range(TILES - 2, TILES + 2):
                turn(t, t % 2)


def kernel(L0_attn_hidden_states, L0_attn_Wq, L0_attn_Wk, L0_attn_Wv, L0_attn_Wo, L0_ffn_A, L0_ffn_B, L0_ffn_Wr,
           L0_ffn_br):
    import numpy as np
    import concourse.bacc as bacc
    from concourse.bass_utils import run_bass_kernel_spmd

    def pair_blocks(w):
        w = np.asarray(w).reshape(KC, P, PAIRS, P)
        return w.transpose(2, 1, 0, 3).reshape(PAIRS, P, KC * P)

    wqkv = np.ascontiguousarray(np.stack([pair_blocks(w) for w in (L0_attn_Wq, L0_attn_Wk, L0_attn_Wv)]))
    a = np.asarray(L0_ffn_A).reshape(HR, EMBED)
    ar = np.concatenate([a, np.asarray(L0_ffn_Wr)], axis=0).T.reshape(KC, P, ARW).transpose(1, 0, 2)
    bt = np.asarray(L0_ffn_B).transpose(0, 2, 1).reshape(HR, EMBED)
    br = np.tile(np.asarray(L0_ffn_br)[None, :], (P, 1))

    inv = (np.float32(1.0) / np.float32(10000.0) ** (np.arange(0, DH, 2, dtype=np.float32) / np.float32(DH)))
    angle = np.tile(np.repeat(inv.astype(np.float32), 2), 2)[:, None] * np.arange(SEQ, dtype=np.float32)[None, :]
    arrays = {
        "x": np.ascontiguousarray(np.asarray(L0_attn_hidden_states).reshape(TOKENS, EMBED)),
        "wqkv": wqkv,
        "wo": np.ascontiguousarray(L0_attn_Wo),
        "ar": np.ascontiguousarray(ar),
        "bt": np.ascontiguousarray(bt),
        "br": np.ascontiguousarray(br),
        "cos": np.cos(angle).astype(np.float32),
        "sin": np.sin(angle).astype(np.float32),
    }
    nc = bacc.Bacc("TRN2", target_bir_lowering=False, num_devices=1)
    args = {n: nc.dram_tensor(f"in_{n}", a.shape, F32, kind="ExternalInput").ap() for n, a in arrays.items()}
    scratch = nc.dram_tensor("attention_out", (HEADS, DH, TOKENS), F32, kind="Internal").ap()
    out = nc.dram_tensor("out", (TOKENS, EMBED), F32, kind="ExternalOutput").ap()
    sandwich_kernel(nc, args["x"], args["wqkv"], args["wo"], args["ar"], args["bt"], args["br"], args["cos"],
                    args["sin"], scratch, out)
    r = run_bass_kernel_spmd(nc, [{f"in_{n}": a for n, a in arrays.items()}], core_ids=[0])
    return r.results[0]["out"].reshape(BATCHES, SEQ, EMBED)
```
